# Optimizing a Trainium2 kernel written in Bass

```python
import numpy as np
import jax
import jax.numpy as jnp

def _softmax(x, axis=-1):
    return jax.nn.softmax(x, axis=axis)

def _gelu(x):
    return jax.nn.gelu(x, approximate=True)

def _silu(x):
    return jax.nn.silu(x)

def _sigmoid(x):
    return jax.nn.sigmoid(x)

def _layernorm(x, axis=-1, eps=1e-05):
    m = jnp.mean(x, axis=axis, keepdims=True)
    v = jnp.var(x, axis=axis, keepdims=True)
    return (x - m) / jnp.sqrt(v + eps)

def _scatter_add(tgt, idx, src, axis=0):
    return tgt.at[idx].add(src)

def _segment_sum(src, seg, n):
    return jax.ops.segment_sum(src, seg, n)
kernel_name = 'mk_sandwich_d1_jaxref_r8_6d38cf'

def setup_inputs(seed: int=0):
    np.random.seed(seed)
    _w = jnp.asarray

    def _L0_attn_setup():
        import jax, jax.numpy as jnp
        import numpy as np
        DIM = 256
        N_HEAD = 16
        N_KV_HEAD = 4
        DQK = 128
        DV = DIM // N_HEAD
        N_REP = N_HEAD // N_KV_HEAD
        WIN = 64
        FRONT = 32
        SEQ = 512
        THETA = 10000.0

        def rope_cos_sin(seq_len, dim, theta=THETA):
            inv_freq = 1.0 / theta ** (np.arange(0, dim, 2)[:dim // 2].astype(np.float32) / dim)
            t = np.arange(seq_len, dtype=np.float32)
            ang = np.outer(t, inv_freq)
            return (jnp.asarray(np.cos(ang)), jnp.asarray(np.sin(ang)))

        def apply_rope(x, cos, sin):
            xr = x[..., 0::2]
            xi = x[..., 1::2]
            c = cos[None, :, None, :]
            s = sin[None, :, None, :]
            out_r = xr * c - xi * s
            out_i = xr * s + xi * c
            return jnp.stack([out_r, out_i], axis=-1).reshape(x.shape)

        def build_mask(seq_len, window, front):
            i = jnp.arange(seq_len)[:, None]
            j = jnp.arange(seq_len)[None, :]
            band = (j <= i) & (j > i - window)
            front_ok = (j < front) & (j <= i - window)
            allowed = band | front_ok
            return jnp.where(allowed, 0.0, -jnp.inf).astype(jnp.float32)
        key = jax.random.key(seed)
        ks = jax.random.split(key, 5)
        B = 1
        scale_in = 1.0 / np.sqrt(DIM)
        x = jax.random.normal(ks[0], (B, SEQ, DIM), dtype=jnp.float32)
        wq = jax.random.normal(ks[1], (DIM, N_HEAD * DQK), dtype=jnp.float32) * scale_in
        wk = jax.random.normal(ks[2], (DIM, N_KV_HEAD * DQK), dtype=jnp.float32) * scale_in
        wv = jax.random.normal(ks[3], (DIM, N_KV_HEAD * DV), dtype=jnp.float32) * scale_in
        wo = jax.random.normal(ks[4], (N_HEAD * DV, DIM), dtype=jnp.float32) * scale_in
        return {'x': x, 'wq': wq, 'wk': wk, 'wv': wv, 'wo': wo}
    _L0_attn_in = _L0_attn_setup()

    def _L0_ffn_setup():
        import jax, jax.numpy as jnp
        import numpy as np
        BLOCK = 64

        def dequant4bit(q, scale):
            return (q.astype(jnp.float32) - 7.5) * jnp.repeat(scale, BLOCK, axis=1)
        key = jax.random.key(seed)
        ks = jax.random.split(key, 11)
        B, S, D, H, R = (4, 256, 256, 1024, 16)
        return {'x1': jax.random.normal(ks[0], (B, S, D), jnp.float32), 'w_up_q': jax.random.randint(ks[1], (H, D), 0, 16, dtype=jnp.int32), 'w_up_scale': jax.random.uniform(ks[2], (H, D // BLOCK), jnp.float32) * 0.02, 'b_up': jax.random.normal(ks[3], (H,), jnp.float32) * 0.01, 'w_up_lora_a': jax.random.normal(ks[4], (D, R), jnp.float32) * 0.02, 'w_up_lora_b': jax.random.normal(ks[5], (R, H), jnp.float32) * 0.02, 'w_down_q': jax.random.randint(ks[6], (D, H), 0, 16, dtype=jnp.int32), 'w_down_scale': jax.random.uniform(ks[7], (D, H // BLOCK), jnp.float32) * 0.02, 'b_down': jax.random.normal(ks[8], (D,), jnp.float32) * 0.01, 'w_down_lora_a': jax.random.normal(ks[9], (H, R), jnp.float32) * 0.02, 'w_down_lora_b': jax.random.normal(ks[10], (R, D), jnp.float32) * 0.02}
    _L0_ffn_in = _L0_ffn_setup()
    _d = {'L0_attn_x': _L0_attn_in['x'], 'L0_attn_wq': _L0_attn_in['wq'], 'L0_attn_wk': _L0_attn_in['wk'], 'L0_attn_wv': _L0_attn_in['wv'], 'L0_attn_wo': _L0_attn_in['wo'], 'L0_ffn_w_up_q': _L0_ffn_in['w_up_q'], 'L0_ffn_w_up_scale': _L0_ffn_in['w_up_scale'], 'L0_ffn_b_up': _L0_ffn_in['b_up'], 'L0_ffn_w_up_lora_a': _L0_ffn_in['w_up_lora_a'], 'L0_ffn_w_up_lora_b': _L0_ffn_in['w_up_lora_b'], 'L0_ffn_w_down_q': _L0_ffn_in['w_down_q'], 'L0_ffn_w_down_scale': _L0_ffn_in['w_down_scale'], 'L0_ffn_b_down': _L0_ffn_in['b_down'], 'L0_ffn_w_down_lora_a': _L0_ffn_in['w_down_lora_a'], 'L0_ffn_w_down_lora_b': _L0_ffn_in['w_down_lora_b']}
    _x0 = _d['L0_attn_x']
    _d['L0_attn_x'] = jax.random.normal(jax.random.fold_in(jax.random.key(seed), 1), (4, 1024, 256), dtype=_x0.dtype)
    del _x0
    return _d

def reference(L0_attn_x, L0_attn_wq, L0_attn_wk, L0_attn_wv, L0_attn_wo, L0_ffn_w_up_q, L0_ffn_w_up_scale, L0_ffn_b_up, L0_ffn_w_up_lora_a, L0_ffn_w_up_lora_b, L0_ffn_w_down_q, L0_ffn_w_down_scale, L0_ffn_b_down, L0_ffn_w_down_lora_a, L0_ffn_w_down_lora_b):

    def _L0_attn_ref(x, wq, wk, wv, wo):
        import jax, jax.numpy as jnp
        import numpy as np
        DIM = 256
        N_HEAD = 16
        N_KV_HEAD = 4
        DQK = 128
        DV = DIM // N_HEAD
        N_REP = N_HEAD // N_KV_HEAD
        WIN = 64
        FRONT = 32
        SEQ = 512
        THETA = 10000.0

        def rope_cos_sin(seq_len, dim, theta=THETA):
            inv_freq = 1.0 / theta ** (np.arange(0, dim, 2)[:dim // 2].astype(np.float32) / dim)
            t = np.arange(seq_len, dtype=np.float32)
            ang = np.outer(t, inv_freq)
            return (jnp.asarray(np.cos(ang)), jnp.asarray(np.sin(ang)))

        def apply_rope(x, cos, sin):
            xr = x[..., 0::2]
            xi = x[..., 1::2]
            c = cos[None, :, None, :]
            s = sin[None, :, None, :]
            out_r = xr * c - xi * s
            out_i = xr * s + xi * c
            return jnp.stack([out_r, out_i], axis=-1).reshape(x.shape)

        def build_mask(seq_len, window, front):
            i = jnp.arange(seq_len)[:, None]
            j = jnp.arange(seq_len)[None, :]
            band = (j <= i) & (j > i - window)
            front_ok = (j < front) & (j <= i - window)
            allowed = band | front_ok
            return jnp.where(allowed, 0.0, -jnp.inf).astype(jnp.float32)
        B, S, _ = x.shape
        q = (x @ wq).reshape(B, S, N_HEAD, DQK)
        k = (x @ wk).reshape(B, S, N_KV_HEAD, DQK)
        v = (x @ wv).reshape(B, S, N_KV_HEAD, DV)
        cos, sin = rope_cos_sin(S, DQK)
        q = apply_rope(q, cos, sin)
        k = apply_rope(k, cos, sin)
        q = q.transpose(0, 2, 1, 3)
        k = k.transpose(0, 2, 1, 3)
        v = v.transpose(0, 2, 1, 3)
        k = jnp.repeat(k, N_REP, axis=1)
        v = jnp.repeat(v, N_REP, axis=1)
        mask = build_mask(S, WIN, FRONT)
        scores = jnp.einsum('bhqd,bhkd->bhqk', q, k) / np.sqrt(DQK).astype(np.float32)
        scores = scores + mask[None, None, :, :]
        attn = jax.nn.softmax(scores, axis=-1)
        out = jnp.einsum('bhqk,bhkd->bhqd', attn, v)
        out = out.transpose(0, 2, 1, 3).reshape(B, S, N_HEAD * DV)
        return out @ wo

    def _L0_ffn_ref(x1, w_up_q, w_up_scale, b_up, w_up_lora_a, w_up_lora_b, w_down_q, w_down_scale, b_down, w_down_lora_a, w_down_lora_b):
        import jax, jax.numpy as jnp
        import numpy as np
        BLOCK = 64

        def dequant4bit(q, scale):
            return (q.astype(jnp.float32) - 7.5) * jnp.repeat(scale, BLOCK, axis=1)
        w_up = dequant4bit(w_up_q, w_up_scale).T
        y1 = x1 @ w_up + b_up + x1 @ w_up_lora_a @ w_up_lora_b
        x2 = jax.nn.relu(y1)
        w_down = dequant4bit(w_down_q, w_down_scale).T
        y2 = x2 @ w_down + b_down + x2 @ w_down_lora_a @ w_down_lora_b
        return y2
    x = L0_attn_x
    x = x + _layernorm(_L0_attn_ref(_layernorm(x, axis=-1), L0_attn_wq, L0_attn_wk, L0_attn_wv, L0_attn_wo), axis=-1)
    x = x + _layernorm(_L0_ffn_ref(_layernorm(x, axis=-1), L0_ffn_w_up_q, L0_ffn_w_up_scale, L0_ffn_b_up, L0_ffn_w_up_lora_a, L0_ffn_w_up_lora_b, L0_ffn_w_down_q, L0_ffn_w_down_scale, L0_ffn_b_down, L0_ffn_w_down_lora_a, L0_ffn_w_down_lora_b), axis=-1)
    return x

_drawn_inputs = setup_inputs


def setup_inputs(seed=0):
    import zlib

    import numpy as np

    out = dict(_drawn_inputs(seed))
    spreads = {}
    factors = {'L0_ffn_b_up': 8.0,
     'L0_ffn_w_up_lora_a': 3.342,
     'L0_ffn_w_up_lora_b': 3.332,
     'L0_ffn_b_down': 8.0,
     'L0_ffn_w_down_lora_a': 3.387,
     'L0_ffn_w_down_lora_b': 3.463}
    for name, (base, spread) in spreads.items():
        noise = np.random.default_rng([zlib.crc32(name.encode()), seed]).standard_normal(out[name].shape)
        drawn = base * np.exp(spread * noise) if base else spread * noise
        out[name] = jnp.asarray(drawn.astype(out[name].dtype))
    for name, factor in factors.items():
        out[name] = (out[name] * factor).astype(out[name].dtype)
    return out
```

```python
from contextlib import ExitStack

import numpy as np

import concourse.bass as bass
from concourse import mybir

F32 = mybir.dt.float32
F32R = mybir.dt.float32r
F16 = mybir.dt.float16
BF16 = mybir.dt.bfloat16
I32 = mybir.dt.int32
ALU = mybir.AluOpType
ACT = mybir.ActivationFunctionType
AX_X = mybir.AxisListType.X

P = 128
B, S, D = 4, 1024, 256
NH, NG, DQK, DV = 16, 4, 128, 16
REP = NH // NG
WIN, FRONT = 64, 32
HID, RANK = 1024, 16
QBLK = 64
THETA = 10000.0
EPS = 1e-5
CH = 512
NC = B * S // CH
HALVES = S // CH
KC = D // P
HC = HID // P
BLK = CH // WIN
KEYS = 2 * WIN + FRONT
SLOTS = NG * BLK // 2
VP = 3 * (DV + 1)
PSCALE = 2.0 ** 14
MASKED = -1e30
ROPES = NG * (REP + 1)

ROPE_ORDER = ([("k", 0)] + [("q", 0, h) for h in range(REP)] + [("k", 1)] + [("q", 1, h) for h in range(REP)]
              + [("k", 2)] + [("q", 2, h) for h in range(REP)] + [("k", 3)] + [("q", 3, h) for h in range(REP)])
ROPE_AT = {tile: n for n, tile in enumerate(ROPE_ORDER)}
PER_CHUNK = {"rope": ROPES, "vt": 1, "vw": 1, "vf": 1, "ot": 2, "wo": 2, "xa": 2, "up": 8,
             "down": 4, "xn": 2, "wt": 3, "wu": 4, "wd": 4}


def rope(*tile):
    return ("rope", ROPE_AT[tile])


NOW, NEXT, LAST, SETUP = 0, 1, -1, "setup"
JOBS = {
    0: [(NOW, rope("q", 1, 0)), (NOW, rope("q", 1, 1))],
    1: [(NOW, ("vw", 0)), (NOW, ("vf", 0)), (NOW, rope("q", 1, 2))],
    2: [(NOW, rope("q", 1, 3)), (NOW, rope("k", 2))],
    3: [(LAST, ("ot", 0)), (LAST, ("ot", 1)), (NOW, rope("q", 2, 0))],
    4: [(LAST, ("wo", 0)), (LAST, ("wo", 1)), (NOW, rope("q", 2, 1))],
    5: [(NOW, rope("q", 2, 2)), (NOW, rope("q", 2, 3))],
    6: [(NOW, rope("k", 3)), (NOW, rope("q", 3, 0))],
    7: [(LAST, ("xa", 0)), (LAST, ("xa", 1)), (NOW, rope("q", 3, 1))],
    8: [(LAST, ("up", 0)), (LAST, ("up", 1)), (NOW, rope("q", 3, 2))],
    9: [(LAST, ("up", 2)), (LAST, ("up", 3)), (NOW, rope("q", 3, 3))],
    10: [(NEXT, ("xn", 0)), (NEXT, ("xn", 1)), (LAST, ("down", 0))],
    11: [(NEXT, rope("k", 0)), (LAST, ("down", 1))],
    12: [(LAST, ("up", 4)), (LAST, ("up", 5)), (NEXT, rope("q", 0, 0))],
    13: [(LAST, ("up", 6)), (LAST, ("up", 7)), (NEXT, rope("q", 0, 1))],
    14: [(NEXT, rope("q", 0, 2)), (LAST, ("down", 2)), (LAST, ("down", 3))],
    15: [(NEXT, rope("q", 0, 3)), (NEXT, ("vt", 0)), (NEXT, rope("k", 1))],
}
SETUP_JOBS = {3: [("wt", 0), ("wt", 1), ("wt", 2)], 5: [("wu", 0)], 6: [("wu", 1)], 7: [("wu", 2)],
              8: [("wu", 3)], 10: [("wd", 0)], 11: [("wd", 1)], 12: [("wd", 2)], 13: [("wd", 3)]}
PROLOGUE = [(NEXT, ("xn", 0)), (NEXT, ("xn", 1)), (NEXT, rope("k", 0))] + [
    (NEXT, rope("q", 0, h)) for h in range(REP)] + [(NEXT, ("vt", 0)), (NEXT, rope("k", 1))]
EPILOGUE = [(LAST, (kind, n)) for kind, n in [("ot", 0), ("ot", 1), ("wo", 0), ("wo", 1), ("xa", 0), ("xa", 1)]
            + [("up", n) for n in range(4)] + [("down", 0), ("down", 1)]
            + [("up", n) for n in range(4, 8)] + [("down", 2), ("down", 3)]]
BANKS = 3
LN = 3
FIRST, MIDDLE, FINAL = "first", "middle", "final"


def jobs_of(body, slot):
    found = [j for j in JOBS[slot] if not (body == FIRST and j[0] == LAST)
             and not (body == FINAL and j[0] == NEXT)]
    if body == FIRST:
        found = [(SETUP, j) for j in SETUP_JOBS.get(slot, [])] + found
    return found


def plan_banks(jobs, before):
    n, plan = len(jobs), []
    held = dict(enumerate(before))
    for i, job in enumerate(jobs):
        bank = (i - n) % BANKS
        plan.append((job, bank, held.get(bank)))
        held[bank] = job
    return plan, [held[b] for b in range(BANKS)]


def older(jobs):
    return [(label if label == SETUP else label - 1, job) for label, job in jobs]


def build(nc, x, wq, wk, wv, wo, up_q, up_scale, b_up, up_a, up_b, down_q, down_scale, b_down,
          down_a, down_b, tables, mask01, mask2, ident32, ident16, out):
    ctx = ExitStack()
    with ctx:
        def sb(name, shape, dt=F32):
            return ctx.enter_context(nc.sbuf_tensor(name, shape, dt))

        def sem(name):
            return ctx.enter_context(nc.semaphore(name))

        wq_hl = [sb(f"wq_{p}", [P, KC, NH * DQK], F32R) for p in "hl"]
        wk_hl = [sb(f"wk_{p}", [P, KC, NG * DQK], F32R) for p in "hl"]
        wv_hl = [sb(f"wv_{p}", [P, KC, NG * DV], F32R) for p in "hl"]
        wo_hl = [sb(f"wo_{p}", [P, 2, D], F32R) for p in "hl"]
        wup_hl = [sb(f"wup_{p}", [P, KC, HID], F32R) for p in "hl"]
        wdn_hl = [sb(f"wdn_{p}", [P, HC, D], F32R) for p in "hl"]
        id32 = sb("id32", [P, P])
        id16 = sb("id16", [P, P], BF16)
        bup = sb("bup", [P, HC])
        bdn = sb("bdn", [P, D])
        scu = sb("scu", [P, HC, D // QBLK])
        scd = sb("scd", [P, KC, HID // QBLK])
        cs = sb("cs", [P, 2, CH])
        m01 = sb("m01", [P, 2, 2 * KEYS], BF16)
        m2 = sb("m2", [P, 2 * KEYS], BF16)
        xa = sb("xa", [P, 4, D])
        xt_hl = [sb(f"xt_{p}", [P, KC, CH], F32R) for p in "hl"]
        turned = sb("turned", [P, 2, CH])
        straight = sb("straight", [P, 2, CH])
        qrot = sb("qrot", [P, 2, BLK, REP, WIN])
        kwin = sb("kwin", [P, NG, BLK, KEYS])
        kfront = sb("kfront", [P, FRONT])
        vt = sb("vt", [4 * DV, WIN + CH])
        vtf = sb("vtf", [4 * DV, 4 * FRONT])
        vwin = sb("vwin", [P, BLK, NG, VP], BF16)
        vfrest = sb("vfrest", [P, 4 * DV])
        vfp = sb("vfp", [P, 3, 4 * DV], BF16)
        vdiag = sb("vdiag", [P, 2, NG, 4 * VP], BF16)
        nmax = sb("nmax", [P, 2, 4])
        prob = sb("prob", [P, 4, KEYS])
        pfront = sb("pfront", [P, 4 * FRONT])
        p_hl = [sb(f"p_{p}", [P, 2, 5 * P], F16) for p in "hl"]
        osum = sb("osum", [P, 4, 4, DV + 1])
        rsum = sb("rsum", [P, 16])
        oall = sb("oall", [P, BLK, P])
        ot_hl = [sb(f"ot_{p}", [P, 2, CH], F32R) for p in "hl"]
        x2_hl = [sb(f"x2_{p}", [P, HC, CH // 2], F32R) for p in "hl"]
        scratch = sb("scratch", [P, 4608])
        zn = scratch[:, 0:1024].rearrange("p (t d) -> p t d", t=4)
        x1 = scratch[:, 1024:2048].rearrange("p (t d) -> p t d", t=4)
        yo = scratch[:, 2048:3072].rearrange("p (t d) -> p t d", t=4)
        x2f = scratch[:, 3072:4096].rearrange("p (b n) -> p b n", b=2)
        vrest = scratch[:, 4096:4608]
        wq_st = scratch[:, 0:2048].rearrange("p (b k n) -> p b k n", b=2, k=KC)
        wk_st = scratch[:, 2048:3072].rearrange("p (k n) -> p k n", k=KC)
        wv_st = scratch[:, 3072:3200].rearrange("p (k n) -> p k n", k=KC)
        wo_st = scratch[:, 3200:3712].rearrange("p (k n) -> p k n", k=2)
        deq = scratch[:, 0:2048]
        upb_st = scratch[:, 2048:3072]
        dnb_st = scratch[:, 3072:3328]
        upa_t = scratch[:, 3328:3584]
        dna_t = scratch[:, 3584:4608]
        upa_st = sb("upa_st", [P, KC, RANK])
        dna_st = sb("dna_st", [P, HC, RANK])
        st = sb("st", [P, 4, 4, 6])
        mv = sb("mv", [P, 4, 4, 2])
        vareps = sb("vareps", [P, 4, 4])
        rstd = sb("rstd", [P, 4, 4])
        minus_half = sb("minus_half", [P, 4])
        minus_mean = sb("minus_mean", [P, 4, 4])
        nmr = sb("nmr", [P, 4, 4])

        ring = [ctx.enter_context(nc.psum_tensor(f"ring{b}", [P, CH], F32)) for b in range(BANKS)]
        ps_s = ctx.enter_context(nc.psum_tensor("ps_s", [P, 2, 512], F32))
        ps_t = ctx.enter_context(nc.psum_tensor("ps_t", [P, 1024], F32))
        ps_v = ctx.enter_context(nc.psum_tensor("ps_v", [P, 512], F32))

        done = {k: sem(f"{k}_done") for k in PER_CHUNK}
        high = {k: sem(f"{k}_high") for k in ("xn", "ot", "xa", "wu", "wd", "vw", "vf")}
        taken = {k: sem(f"{k}_taken") for k in PER_CHUNK}
        swapped = sem("halves_swapped")
        sin_done = sem("sines_applied")
        rot_done = sem("tiles_rotated")
        k_step = sem("key_steps")
        s_done = sem("scores_done")
        max_done = sem("maxima_done")
        exp_done = sem("exp_done")
        pf_done = sem("front_probs_gathered")
        t_done = sem("prob_transposed")
        ph_done = sem("prob_high_done")
        pl_done = sem("prob_low_done")
        pv_done = sem("pv_done")
        os_done = sem("pv_summed")
        r_done = sem("sums_inverted")
        o_done = sem("heads_normalised")
        v_carry = sem("value_carried")
        v_step = sem("value_parts")
        ln_step = [sem(f"ln{i}_steps") for i in range(4)]
        rstd_done = [sem(f"ln{i}_rstd") for i in range(4)]
        shift_done = {i: sem(f"ln{i}_shift") for i in (1, 3)}
        xn_done = sem("x_normalised")
        z_done = sem("attention_normalised")
        x1_done = sem("x1_done")
        x1n_done = sem("x1_normalised")
        x2h_done = sem("hidden_high_done")
        x2l_done = sem("hidden_low_done")
        y_norm = sem("network_normalised")
        x1_free = sem("x1_free")
        stored = [sem(f"stored{i}") for i in range(2)]
        ld_x = sem("x_loaded")
        ld_x1 = sem("x_reloaded")
        ld_cs = sem("tables_loaded")
        ld_m = sem("masks_loaded")
        ld_w = {k: sem(f"{k}_loaded") for k in ("wk", "wq0", "wq1", "wq2", "wq3", "wv", "wo", "ident",
                                                 "small", "upq", "downq", "rank")}
        w_hi = sem("weights_high")
        w_lo = sem("weights_low")
        fill_step = sem("fill_steps")
        gates = {e.engine: sem(f"gate{i}") for i, e in enumerate((nc.tensor, nc.vector, nc.gpsimd))}
        zeroed = sem("zeroed")
        padded = sem("factors_zeroed")
        deq_done = sem("dequantised")
        WSEQ = ["wk", "wq0", "wv", "wq1", "wq2", "wq3", "wo"]

        x_v = x.rearrange("b (c t p) d -> (b c) p t d", p=P, t=4)
        out_v = out.rearrange("b (c f t p) d -> (b c) f p t d", p=P, f=2, t=2)

        def count(c, label, kind, n):
            if label == SETUP:
                return n + 1
            per = PER_CHUNK[kind]
            return c * per + (label * per + n + 1)

        def half_of(c, label):
            return (c + label) % HALVES

        def sets(c, n):
            return c * SLOTS + (n + 1)

        def over_chunks(e, body_of):
            body_of(0, FIRST)
            with e.Fori(1, NC - 1) as c:
                body_of(c, MIDDLE)
            body_of(NC - 1, FINAL)

        def planned(body):
            jobs = [j for n in range(SLOTS) for j in jobs_of(body, n)]
            plan, tail = plan_banks(jobs, older(PROLOGUE[-BANKS:]))
            by_slot, at = [], 0
            for n in range(SLOTS):
                k = len(jobs_of(body, n))
                by_slot.append(plan[at:at + k])
                at += k
            return by_slot, tail

        prologue = plan_banks(PROLOGUE, [None] * BANKS)[0]
        tail = planned(FINAL)[1]
        epilogue = plan_banks(EPILOGUE, older(tail))[0]

        def held(e, q, value):
            e.wait_ge(q, value)
            e.sem_inc(gates[e.engine], 1)

        block = ctx.enter_context(nc.Block())

        @block.sync
        def _(sp):
            def load_x(c, waited):
                if waited:
                    sp.wait_ge(done["xn"], count(c, NOW, "xn", 1))
                    sp.dma_start(xa[:, :, :], x_v[bass.ds(c + 1, 1)].rearrange("a p t d -> p (a t) d")).then_inc(ld_x, 16)
                else:
                    sp.dma_start(xa[:, :, :], x_v[0]).then_inc(ld_x, 16)

            def load_tables(c, label):
                src = tables[bass.ds(half_of(c, label), 1)] if not isinstance(c, int) else \
                    tables[half_of(c, label):half_of(c, label) + 1]
                sp.dma_start(cs[:, :, :], src.rearrange("a p t n -> p (a t) n")).then_inc(ld_cs, 16)

            def load_masks(c, label):
                src = mask01[bass.ds(half_of(c, label), 1)] if not isinstance(c, int) else \
                    mask01[half_of(c, label):half_of(c, label) + 1]
                sp.dma_start(m01[:, :, :], src.rearrange("a p t n -> p (a t) n")).then_inc(ld_m, 16)

            def load_wq(g):
                if g >= 2:
                    sp.wait_ge(w_lo, WSEQ.index(f"wq{g - 2}") + 1)
                sp.dma_start(wq_st[:, g % 2, :, :],
                             wq.rearrange("(k p) n -> p k n", p=P)[:, :, g * 512:(g + 1) * 512]
                             ).then_inc(ld_w[f"wq{g}"], 16)

            def store(c, f):
                sp.wait_ge(x1_free, c * 2 + (f - 2 + 2))
                at = out_v[bass.ds(c - 1, 1), f].rearrange("a p t d -> p (a t) d")
                sp.dma_start(at, yo[:, 2 * f:2 * f + 2, :]).then_inc(stored[f], 16)

            def setup_loads():
                for q in stored:
                    sp.sem_inc(q, 16)
                load_x(0, False)
                sp.dma_start(id32[:, :], ident32).then_inc(ld_w["ident"], 16)
                sp.dma_start(id16[:, :], ident16).then_inc(ld_w["ident"], 16)
                sp.dma_start(wk_st, wk.rearrange("(k p) n -> p k n", p=P)).then_inc(ld_w["wk"], 16)
                load_wq(0)
                load_tables(0, NOW)
                sp.dma_start(wv_st, wv.rearrange("(k p) n -> p k n", p=P)).then_inc(ld_w["wv"], 16)
                load_masks(0, NOW)
                sp.dma_start(m2[:, :], mask2).then_inc(ld_w["ident"], 16)
                load_wq(1)
                for hh in range(2):
                    sp.dma_start(wo_st[:, hh, :], wo.rearrange("(a hh d) n -> hh a d n", hh=2, d=DV)[hh]
                                 ).then_inc(ld_w["wo"], 16)
                sp.dma_start(bup[:, :], b_up.rearrange("(k p) -> p k", p=P), allow_slow_non_contiguous=True
                             ).then_inc(ld_w["small"], 16)
                sp.dma_start(bdn[:, :], b_down.rearrange("(a n) -> a n", a=1).broadcast_to([P, D])).then_inc(ld_w["small"], 16)
                sp.dma_start(scu[:, :, :], up_scale.rearrange("(k p) n -> p k n", p=P)).then_inc(ld_w["small"], 16)
                sp.dma_start(scd[:, :, :], down_scale.rearrange("(k p) n -> p k n", p=P)).then_inc(ld_w["small"], 16)
                sp.dma_start(upa_st[:, :, :], up_a.rearrange("(k p) n -> p k n", p=P)).then_inc(ld_w["small"], 16)
                sp.dma_start(dna_st[:, :, :], down_a.rearrange("(k p) n -> p k n", p=P)).then_inc(ld_w["small"], 16)
                load_wq(2)
                load_wq(3)

            def setup_loads_late():
                sp.wait_ge(w_lo, len(WSEQ))
                sp.dma_start(deq.bitcast(I32).rearrange("p (k n) -> p k n", k=HC),
                             up_q.rearrange("(k p) n -> p k n", p=P)).then_inc(ld_w["upq"], 16)
                sp.wait_ge(padded, 1)
                sp.dma_start(upb_st[0:RANK, :], up_b).then_inc(ld_w["rank"], 16)
                sp.dma_start(dnb_st[0:RANK, :], down_b).then_inc(ld_w["rank"], 16)

            def setup_loads_last():
                sp.wait_ge(done["wu"], 4)
                sp.dma_start(deq.bitcast(I32).rearrange("p (k n) -> p k n", k=KC),
                             down_q.rearrange("(k p) n -> p k n", p=P)).then_inc(ld_w["downq"], 16)

            def body_of(c, body):
                if body != FINAL:
                    load_x(c, True)
                if body == FIRST:
                    setup_loads_late()
                    setup_loads_last()
                else:
                    sp.wait_ge(x1_free, c * 2 - 1)
                    sp.dma_start(x1, x_v[bass.ds(c - 1, 1)].rearrange("a p t d -> p (a t) d")
                                 ).then_inc(ld_x1, 16)
                if body != FINAL:
                    sp.wait_ge(taken["rope"], count(c, NOW, "rope", ROPES - 1))
                    sp.wait_ge(sin_done, count(c, NOW, "rope", ROPES - 1))
                    load_tables(c, NEXT)
                if body != FIRST:
                    store(c, 0)
                if body != FINAL:
                    sp.wait_ge(s_done, sets(c, SLOTS - 4))
                    load_masks(c, NEXT)
                if body != FIRST:
                    store(c, 1)

            setup_loads()
            over_chunks(sp, body_of)
            sp.wait_ge(x1_free, NC * 2 - 1)
            sp.dma_start(x1, x_v[NC - 1]).then_inc(ld_x1, 16)
            store(NC, 0)
            store(NC, 1)
            for q in stored:
                sp.wait_ge(q, 16 * (NC + 1))

        @block.tensor
        def _(pe):
            PASSES = ((0, 0), (0, 1), (1, 0))

            def claim(c, before):
                if before is not None:
                    label, (kind, n) = before
                    held(pe, taken[kind], count(c, label, kind, n))

            def scores(c, n, body):
                g, s = divmod(n, NG)
                if s == 0:
                    pe.wait_ge(k_step, c * (4 * NG) + 4 * g + 4)
                    pe.wait_ge(rot_done, count(c, NOW, *rope("q", g, REP - 1)))
                if n == 0:
                    pe.wait_ge(ld_m, c * 16 + 16)
                if body != FIRST or n:
                    pe.wait_ge(exp_done, sets(c, n - 1))
                for bb in range(2):
                    blk = 2 * s + bb
                    mask = m01[:, bb, :] if s == 0 else m2[:, :]
                    pe.matmul(ps_s[:, bb, 0:2 * KEYS], id16[:, :], mask, start=True, stop=False,
                              skip_group_check=True)
                    for pr in range(2):
                        mm = pe.matmul(ps_s[:, bb, pr * KEYS:(pr + 1) * KEYS],
                                       qrot[:, g % 2, blk, 2 * pr:2 * pr + 2, :].rearrange("p r q -> p (r q)"),
                                       kwin[:, g, blk, :],
                                       start=False, stop=True, skip_group_check=True)
                mm.then_inc(s_done, 1)

            def transposes(c, m, body):
                pe.wait_ge(exp_done, sets(c, m))
                if body != FIRST or m:
                    pe.wait_ge(pl_done, sets(c, m - 1))
                for k in range(4):
                    pe.transpose(ps_t[:, k * P:(k + 1) * P], prob[:, k, 0:P], id32[:, :])
                pe.wait_ge(pf_done, sets(c, m))
                pe.transpose(ps_t[:, 4 * P:5 * P], pfront[:, :], id32[:, :]).then_inc(t_done, 1)

            def values(c, m, body):
                g, s = divmod(m % SLOTS, NG)
                pe.wait_ge(pl_done, sets(c, m))
                if body != FIRST or m:
                    pe.wait_ge(os_done, sets(c, m - 1))
                if m == 0:
                    pe.wait_ge(v_step, c * 7 + 7)
                lo = 2 * (DV + 1)
                ph, pl = (t[:, m % 2, :] for t in p_hl)
                diag = vdiag[:, 0, g, :]
                pe.matmul(ps_v[:, 0:4 * VP], ph[:, 4 * P:5 * P], diag, start=True, stop=False,
                          skip_group_check=True)
                pe.matmul(ps_v[:, 0:4 * VP].rearrange("p (k n) -> p k n", n=VP)[:, :, 0:lo], pl[:, 4 * P:5 * P],
                          diag.rearrange("p (k n) -> p k n", n=VP)[:, :, 0:lo], start=False, stop=False,
                          skip_group_check=True)
                for k in range(4):
                    w = vwin[:, 2 * s + k // 2, g, :]
                    pe.matmul(ps_v[:, k * VP:(k + 1) * VP], ph[:, k * P:(k + 1) * P], w,
                              start=False, stop=False, skip_group_check=True)
                    mm = pe.matmul(ps_v[:, k * VP:k * VP + lo], pl[:, k * P:(k + 1) * P], w[:, 0:lo],
                                   start=False, stop=True, skip_group_check=True)
                mm.then_inc(pv_done, 1)

            def three_passes(to, terms, start=True):
                for i, (a, b) in enumerate(terms):
                    for j, (pa, pb) in enumerate(PASSES):
                        mm = pe.matmul(to, a[pa], b[pb], start=start and i == 0 and j == 0,
                                       stop=i == len(terms) - 1 and j == len(PASSES) - 1)
                return mm

            def job(c, plan):
                (label, (kind, n)), bank, before = plan
                claim(c, before)
                to = ring[bank]
                if kind == "rope":
                    tile = ROPE_ORDER[n]
                    if n == 0:
                        pe.wait_ge(taken["xn"], count(c, label, "xn", KC - 1))
                    if isinstance(c, int) and c + label == 0:
                        name = "wk" if tile[0] == "k" else f"wq{tile[1]}"
                        pe.wait_ge(w_lo, WSEQ.index(name) + 1)
                    if tile[0] == "k":
                        w, at = wk_hl, tile[1] * DQK
                    else:
                        w, at = wq_hl, (tile[1] * REP + tile[2]) * DQK
                    mm = three_passes(to[:, :], [([t[:, k, at:at + DQK] for t in w], [t[:, k, :] for t in xt_hl])
                                                 for k in range(KC)])
                elif kind == "xn":
                    pe.wait_ge(xn_done, c * 1 + (label + 1))
                    if isinstance(c, int) and c < 0:
                        pe.wait_ge(ld_w["ident"], 48)
                    for t in range(4):
                        mm = pe.transpose(to[:, t * P:(t + 1) * P], xa[:, t, n * P:(n + 1) * P], id32[:, :])
                elif kind == "vt":
                    if isinstance(c, int) and c < 0:
                        pe.wait_ge(w_lo, WSEQ.index("wv") + 1)
                    mm = three_passes(to[0:NG * DV, :], [([t[:, k, :] for t in wv_hl], [t[:, k, :] for t in xt_hl])
                                                         for k in range(KC)])
                elif kind == "vw":
                    held(pe, taken["vt"], count(c, label, "vt", 0))
                    for w in range(BLK):
                        mm = pe.transpose(to[:, w * 64:(w + 1) * 64], vt[:, w * WIN:(w + 2) * WIN],
                                          id32[0:64, 0:64])
                elif kind == "vf":
                    mm = pe.transpose(to[:, 0:64], vtf[:, :], id32[0:64, 0:64])
                elif kind == "ot":
                    pe.wait_ge(o_done, c * NG + (label + 1) * NG)
                    for b in range(4):
                        mm = pe.transpose(to[:, b * P:(b + 1) * P], oall[:, 4 * n + b, :], id32[:, :])
                elif kind == "wo":
                    if n == 0:
                        pe.wait_ge(taken["ot"], count(c, label, "ot", 1))
                    for i in range(2):
                        t = 2 * n + i
                        mm = three_passes(to[:, i * D:(i + 1) * D],
                                          [([o[:, hh, t * P:(t + 1) * P] for o in ot_hl], [w[:, hh, :] for w in wo_hl])
                                           for hh in range(2)])
                elif kind == "xa":
                    pe.wait_ge(x1n_done, c * 2 + (2 * label + 2))
                    for t in range(4):
                        mm = pe.transpose(to[:, t * P:(t + 1) * P], zn[:, t, n * P:(n + 1) * P], id32[:, :])
                elif kind == "up":
                    if n == 0:
                        pe.wait_ge(taken["xa"], count(c, label, "xa", 1))
                    f, h0 = n // 4, 2 * (n % 4)
                    for i in range(2):
                        at = (h0 + i) * P
                        mm = three_passes(to[:, i * 256:(i + 1) * 256],
                                          [([w[:, k, at:at + P] for w in wup_hl],
                                            [o[:, k, f * 256:(f + 1) * 256] for o in ot_hl]) for k in range(KC)])
                elif kind == "down":
                    pe.wait_ge(x2l_done, count(c, label, "up", 4 * (n // 2) + 3))
                    i = n % 2
                    mm = three_passes(to[:, 0:D], [([o[:, k, i * P:(i + 1) * P] for o in x2_hl],
                                                    [w[:, k, :] for w in wdn_hl]) for k in range(HC)])
                elif kind == "wt":
                    pe.wait_ge(ld_w["small"], 96)
                    blocks = [upa_st[:, k, :] for k in range(KC)] if n == 0 else \
                        [dna_st[:, 4 * (n - 1) + k, :] for k in range(4)]
                    for i, a in enumerate(blocks):
                        mm = pe.transpose(to[0:RANK, i * P:(i + 1) * P], a, id32[:, :])
                elif kind == "wu":
                    if n == 0:
                        pe.wait_ge(taken["wt"], 3)
                        pe.wait_ge(ld_w["rank"], 32)
                        pe.wait_ge(deq_done, 1)
                    k, hh = n // 2, n % 2
                    pe.matmul(to[:, :], upa_t[:, k * P:(k + 1) * P], upb_st[:, hh * 512:(hh + 1) * 512],
                              start=True, stop=False, skip_group_check=True)
                    for i in range(4):
                        t = deq.rearrange("p (k n) -> p k n", k=HC)[:, 4 * hh + i, k * P:(k + 1) * P]
                        mm = pe.matmul(to[:, i * P:(i + 1) * P], t, id32[:, :], start=False, stop=True,
                                       skip_group_check=True)
                elif kind == "wd":
                    if n == 0:
                        pe.wait_ge(deq_done, 2)
                    for i in range(2):
                        h = 2 * n + i
                        pe.matmul(to[:, i * D:(i + 1) * D], dna_t[:, h * P:(h + 1) * P], dnb_st[:, :],
                                  start=i == 0, stop=False, skip_group_check=True)
                        for o in range(KC):
                            t = deq.rearrange("p (k n) -> p k n", k=KC)[:, o, h * P:(h + 1) * P]
                            mm = pe.matmul(to[:, i * D + o * P:i * D + (o + 1) * P], t, id32[:, :],
                                           start=False, stop=True, skip_group_check=True)
                mm.then_inc(done[kind], 1)

            def body_of(c, body):
                slots, _ = planned(body)
                for n in range(SLOTS):
                    scores(c, n, body)
                    if body != FIRST or n >= 1:
                        transposes(c, n - 1, body)
                    if n == 1 and body != FIRST:
                        values(c, n - 2, body)
                    for plan in slots[n]:
                        job(c, plan)
                    if n >= 2 or (n == 0 and body != FIRST):
                        values(c, n - 2, body)

            for plan in prologue:
                job(-1, plan)
            over_chunks(pe, body_of)
            transposes(NC - 1, SLOTS - 1, FINAL)
            values(NC - 1, SLOTS - 2, FINAL)
            values(NC - 1, SLOTS - 1, FINAL)
            for plan in epilogue:
                job(NC, plan)

        def hi_lo(kind, n, bank):
            to = ring[bank][:, :]
            if kind == "xn":
                return [t[:, n, :] for t in xt_hl], to
            if kind == "xa":
                return [t[:, n, :] for t in ot_hl], to
            if kind == "ot":
                return [t[:, :, n * 256:(n + 1) * 256].rearrange("p h (b q) -> p b h q", q=WIN) for t in ot_hl], \
                    to.rearrange("p (b h q) -> p b h q", b=4, h=2)
            if kind == "wu":
                return [t[:, n // 2, (n % 2) * 512:(n % 2 + 1) * 512] for t in wup_hl], to
            return [t[:, 2 * n:2 * n + 2, :] for t in wdn_hl], to.rearrange("p (k n) -> p k n", k=2)

        def weight(name):
            if name[:2] == "wv":
                return [(wv_st[:, k, :], [t[:, k, :] for t in wv_hl]) for k in range(KC)]
            if name[:2] == "wo":
                return [(wo_st[:, k, :], [t[:, k, :] for t in wo_hl]) for k in range(2)]
            if name[:2] == "wk":
                src, parts, at = wk_st, wk_hl, 0
            else:
                g = int(name[2])
                src, parts, at = wq_st[:, g % 2, :, :], wq_hl, g * 512
            return [(src[:, k, :].rearrange("p (h f t) -> p h t f", h=4, t=2),
                     [t[:, k, at:at + 512].rearrange("p (h t f) -> p h t f", h=4, t=2) for t in parts])
                    for k in range(KC)]

        @block.scalar
        def _(act):
            def exp(c, n):
                act.wait_ge(max_done, sets(c, n))
                if not (isinstance(c, int) and c == 0 and n == 0):
                    act.wait_ge(t_done, sets(c, n - 1))
                for k in range(4):
                    e = nc.scalar.activation(prob[:, k, :],
                                             ps_s[:, k // 2, (k % 2) * KEYS:(k % 2 + 1) * KEYS],
                                             ACT.Exp, bias=nmax[:, n % 2, k:k + 1])
                e.then_inc(exp_done, 1)

            def prob_high(c, m):
                act.wait_ge(t_done, sets(c, m))
                nc.scalar.activation(p_hl[0][:, m % 2, :], ps_t[:, 0:5 * P], ACT.Copy, scale=PSCALE
                                     ).then_inc(ph_done, 1)

            def split_weight(name):
                i = WSEQ.index(name)
                act.wait_ge(ld_w[name], 32 if name == "wo" else 16)
                for src, parts in weight(name):
                    e = nc.scalar.activation(parts[0], src, ACT.Copy)
                e.then_inc(w_hi, 1)

            def item(c, plan):
                (label, (kind, n)), bank, _ = plan
                ps = ring[bank]
                act.wait_ge(done[kind], count(c, label, kind, n))
                if kind == "rope":
                    if not (isinstance(c, int) and c + label == 0 and n < 2):
                        act.wait_ge(rot_done, count(c, label, kind, n - 2))
                    nc.scalar.activation(turned[0:64, n % 2, :], ps[64:128, :], ACT.Copy)
                    nc.scalar.activation(turned[64:128, n % 2, :], ps[0:64, :], ACT.Copy).then_inc(swapped, 1)
                elif kind == "vt":
                    if isinstance(c, int) and c < 0:
                        act.wait_ge(zeroed, 1)
                    else:
                        nc.scalar.activation(vt[:, 0:WIN], vt[:, CH:CH + WIN], ACT.Copy).then_inc(v_carry, 1)
                        act.wait_ge(v_carry, c + (label + 0))
                    nc.scalar.activation(vtf[:, :].rearrange("p (k n) -> p k n", k=4),
                                         ps[0:64, 0:FRONT].unsqueeze(1).broadcast_to([64, 4, FRONT]), ACT.Copy)
                    nc.scalar.activation(vt[:, WIN:], ps[0:64, :], ACT.Copy).then_inc(taken["vt"], 1)
                elif kind == "vw":
                    nc.scalar.activation(vwin[:, :, :, 0:DV], ps[:, :].rearrange("p (w g d) -> p w g d", g=NG, d=DV),
                                         ACT.Copy).then_inc(high["vw"], 1)
                elif kind == "vf":
                    nc.scalar.activation(vfp[:, 0, :], ps[:, 0:64], ACT.Copy).then_inc(high["vf"], 1)
                elif kind == "wo":
                    act.wait_ge(shift_done[1], count(c, label, "wo", n))
                    for i in range(2):
                        t = 2 * n + i
                        e = nc.scalar.activation(zn[:, t, :], ps[:, i * D:(i + 1) * D], ACT.Identity,
                                                 bias=nmr[:, 1, t:t + 1], scale=rstd[:, 1, t:t + 1])
                    e.then_inc(taken["wo"], 1)
                elif kind == "up":
                    if n >= 2:
                        act.wait_ge(x2l_done, count(c, label, kind, n - 2))
                    for i in range(2):
                        h = 2 * (n % 4) + i
                        e = nc.scalar.activation(x2f[:, n % 2, i * 256:(i + 1) * 256], ps[:, i * 256:(i + 1) * 256],
                                                 ACT.Relu, bias=bup[:, h:h + 1])
                    e.then_inc(taken["up"], 1)
                elif kind == "wt":
                    act.wait_ge(padded, 1)
                    if n == 0:
                        nc.scalar.activation(upa_t[0:RANK, :], ps[0:RANK, 0:256], ACT.Copy).then_inc(taken["wt"], 1)
                    else:
                        nc.scalar.activation(dna_t[0:RANK, (n - 1) * 512:n * 512], ps[0:RANK, :], ACT.Copy
                                             ).then_inc(taken["wt"], 1)
                else:
                    parts, src = hi_lo(kind, n, bank)
                    nc.scalar.activation(parts[0], src, ACT.Copy).then_inc(high[kind], 1)

            def normalise_y(c, label, n):
                act.wait_ge(shift_done[3], c * 2 + (2 * label + n + 1))
                for i in range(2):
                    t = 2 * n + i
                    e = nc.scalar.activation(yo[:, t, :], yo[:, t, :], ACT.Identity,
                                             bias=nmr[:, 3, t:t + 1], scale=rstd[:, 3, t:t + 1])
                e.then_inc(y_norm, 1)

            def body_of(c, body):
                slots, _ = planned(body)
                for n in range(SLOTS):
                    if body != FIRST or n:
                        prob_high(c, n - 1)
                    exp(c, n)
                    if n:
                        for (label, (kind, k)), _, _ in slots[n - 1]:
                            if kind == "down" and k % 2:
                                normalise_y(c, label, k // 2)
                    for plan in sorted(slots[n], key=lambda plan: plan[0][1][0] == "wo"):
                        if plan[0][1][0] != "down":
                            item(c, plan)

            act.wait_ge(ld_w["small"], 96)
            for name in ("wk", "wq0", "wv"):
                split_weight(name)
            for plan in prologue:
                item(-1, plan)
            for name in WSEQ[3:]:
                split_weight(name)
            over_chunks(act, body_of)
            prob_high(NC - 1, SLOTS - 1)
            for plan in epilogue:
                kind, n = plan[0][1]
                if kind != "down":
                    item(NC, plan)
                elif n % 2:
                    normalise_y(NC, LAST, n // 2)

        @block.vector
        def _(dve):
            V = nc.vector

            def maxima(c, n):
                dve.wait_ge(s_done, sets(c, n))
                V.tensor_reduce(nmax[:, n % 2, :].rearrange("p (b r) -> p b r", b=2),
                                ps_s[:, :, 0:2 * KEYS].rearrange("p b (r k) -> p b r k", r=2),
                                AX_X, ALU.max, negate=True).then_inc(max_done, 1)

            def prob_low(c, m):
                dve.wait_ge(ph_done, sets(c, m))
                V.scalar_tensor_tensor(p_hl[1][:, m % 2, :], ps_t[:, 0:5 * P], PSCALE, p_hl[0][:, m % 2, :],
                                       ALU.mult, ALU.subtract).then_inc(pl_done, 1)

            def sum_parts(c, m, body):
                m = m % SLOTS if m >= 0 else m
                g, s = divmod(m % SLOTS, NG)
                dve.wait_ge(pv_done, sets(c, m))
                if s == 0 and not (body == FIRST and m == 0):
                    dve.wait_ge(o_done, c * NG + (m // NG))
                V.tensor_reduce(osum[:, s, :, :], ps_v[:, 0:4 * VP].rearrange("p (k a n) -> p k n a", k=4, a=3),
                                AX_X, ALU.add).then_inc(os_done, 1)

            def normalise_heads(c, m, body):
                m = m % SLOTS if m >= 0 else m
                g, s = divmod(m % SLOTS, NG)
                if s < NG - 1:
                    return
                dve.wait_ge(os_done, sets(c, m))
                all16 = osum[:, :, :, :].rearrange("p s k n -> p (s k) n")
                V.reciprocal(rsum[:, :].unsqueeze(2), all16[:, :, DV:DV + 1]).then_inc(r_done, 1)
                dve.wait_ge(r_done, c * NG + (m // NG + 1))
                if g == 0 and body != FIRST:
                    dve.wait_ge(done["ot"], count(c, LAST, "ot", 1))
                V.tensor_tensor(oall[:, :, g * 32:(g + 1) * 32].rearrange("p b (r d) -> p b r d", r=2),
                                all16[:, :, 0:DV].rearrange("p (b r) d -> p b r d", r=2),
                                rsum[:, :].rearrange("p (b r) -> p b r", r=2).unsqueeze(3).broadcast_to([P, BLK, 2, DV]),
                                ALU.mult).then_inc(o_done, 1)

            def ln_stats(i, srcs, t0, before):
                q, n = ln_step[i], len(srcs)
                for t, src in enumerate(srcs):
                    e = V.bn_stats(st[:, i, t0 + t, :], src)
                e.then_inc(q, 1)
                held(dve, q, before + 1)
                for t in range(n):
                    e = V.bn_aggr(mv[:, i, t0 + t, :], st[:, i, t0 + t, :])
                e.then_inc(q, 1)
                dve.wait_ge(q, before + 2)
                if i in shift_done:
                    V.tensor_scalar(minus_mean[:, i, t0:t0 + n].unsqueeze(2), mv[:, i, t0:t0 + n, 0:1], -1.0, None,
                                    ALU.mult)
                V.tensor_scalar(vareps[:, i, t0:t0 + n].unsqueeze(2), mv[:, i, t0:t0 + n, 1:2], EPS, None,
                                ALU.add).then_inc(q, 1)

            def normalise(i, to, src, t):
                return V.tensor_scalar(to, src, mv[:, i, t, 0:1], rstd[:, i, t:t + 1], ALU.subtract, ALU.mult)

            def stats_x(c, label):
                dve.wait_ge(ld_x, c * 16 + 16 * (label + 1))
                ln_stats(0, [xa[:, t, :] for t in range(4)], 0, c * LN + LN * label)

            def norm_x(c, label):
                dve.wait_ge(rstd_done[0], c + (label + 1))
                for t in range(4):
                    e = normalise(0, xa[:, t, :], xa[:, t, :], t)
                e.then_inc(xn_done, 1)

            def stats_x1(c):
                for f in range(2):
                    dve.wait_ge(x1_done, c * 2 + (2 * LAST + f + 1))
                    ln_stats(2, [x1[:, 2 * f + i, :] for i in range(2)], 2 * f, c * (2 * LN) + (2 * LAST + f) * LN)

            def norm_x1(c):
                for f in range(2):
                    dve.wait_ge(rstd_done[2], c * 2 + (2 * LAST + f + 1))
                    for i in range(2):
                        t = 2 * f + i
                        e = normalise(2, zn[:, t, :], x1[:, t, :], t)
                    e.then_inc(x1n_done, 1)

            def split_weight(name):
                i = WSEQ.index(name)
                dve.wait_ge(w_hi, i + 1)
                for src, parts in weight(name):
                    e = V.tensor_tensor(parts[1], src, parts[0], ALU.subtract)
                e.then_inc(w_lo, 1)

            def dequant(n):
                q, w = (up_q, down_q)[n], deq.bitcast(I32)
                dve.wait_ge(ld_w[("upq", "downq")[n]], 16)
                dve.wait_ge(ld_w["small"], 96)
                tiles, sc = ((HC, scu), (KC, scd))[n]
                wide = 2048 // tiles
                for k in range(tiles):
                    v = w[:, k * wide:(k + 1) * wide].rearrange("p (b n) -> p b n", n=QBLK)
                    o = deq[:, k * wide:(k + 1) * wide].rearrange("p (b n) -> p b n", n=QBLK)
                    e = V.scalar_tensor_tensor(o, v, -7.5, sc[:, k, :].unsqueeze(2).broadcast_to([P, wide // QBLK, QBLK]),
                                               ALU.add, ALU.mult)
                e.then_inc(deq_done, 1)

            def cosines(c, label, n, bank):
                dve.wait_ge(swapped, count(c, label, "rope", n))
                if n == 0:
                    dve.wait_ge(ld_cs, c * 16 + 16 * (label + 1))
                if not (isinstance(c, int) and c + label == 0 and n < 2):
                    dve.wait_ge(rot_done, count(c, label, "rope", n - 2))
                V.tensor_tensor(straight[:, n % 2, :], ring[bank][:, :], cs[:, 0, :], ALU.mult
                                ).then_inc(taken["rope"], 1)

            def rotate(c, label, n):
                tile = ROPE_ORDER[n]
                g = tile[1]
                dve.wait_ge(sin_done, count(c, label, "rope", n))
                dve.wait_ge(taken["rope"], count(c, label, "rope", n))
                first = isinstance(c, int) and c + label == 0
                if tile[0] == "q":
                    if not (first and g < 2):
                        dve.wait_ge(s_done, c * SLOTS + (label * SLOTS + NG * g - NG))
                    V.tensor_tensor(qrot[:, g % 2, :, tile[2], :],
                                    straight[:, n % 2, :].rearrange("p (b n) -> p b n", n=WIN),
                                    turned[:, n % 2, :].rearrange("p (b n) -> p b n", n=WIN),
                                    ALU.add).then_inc(rot_done, 1)
                    return
                k4 = c * (4 * NG) + (label * 4 * NG + 4 * g)
                own = kwin[:, g, :, WIN:2 * WIN]
                if not first:
                    dve.wait_ge(s_done, c * SLOTS + (label * SLOTS - SLOTS + NG * g + NG))
                    V.tensor_copy(kwin[:, g, 0, 0:WIN], own[:, BLK - 1, :]).then_inc(k_step, 1)
                else:
                    V.memset(kwin[:, g, 0, 0:WIN], 0.0).then_inc(k_step, 1)
                if not (first and g == 0):
                    dve.wait_ge(k_step, k4)
                V.tensor_tensor(kfront[:, :], straight[:, n % 2, 0:FRONT], turned[:, n % 2, 0:FRONT], ALU.add
                                ).then_inc(k_step, 1)
                dve.wait_ge(k_step, k4 + 2)
                half = half_of(c, label)
                if isinstance(c, int):
                    to = kwin[:, g, :, (2 - half) * WIN:(2 - half) * WIN + FRONT]
                else:
                    to = kwin[:, g, :, bass.ds(half * (-WIN) + 2 * WIN, FRONT)]
                V.tensor_scalar(to, kfront[:, :].unsqueeze(1).broadcast_to([P, BLK, FRONT]), 1.0, None, ALU.mult
                                ).then_inc(k_step, 1)
                dve.wait_ge(k_step, k4 + 3)
                V.tensor_tensor(own, straight[:, n % 2, :].rearrange("p (b n) -> p b n", n=WIN),
                                turned[:, n % 2, :].rearrange("p (b n) -> p b n", n=WIN), ALU.add
                                ).then_inc(rot_done, 1)
                dve.wait_ge(rot_done, count(c, label, "rope", n))
                V.tensor_copy(kwin[:, g, 1:BLK, 0:WIN], own[:, 0:BLK - 1, :]).then_inc(k_step, 1)

            def item(c, plan):
                (label, (kind, n)), bank, _ = plan
                ps = ring[bank]
                if kind == "rope":
                    cosines(c, label, n, bank)
                elif kind in ("xn", "ot", "xa", "wu", "wd"):
                    dve.wait_ge(high[kind], count(c, label, kind, n))
                    parts, src = hi_lo(kind, n, bank)
                    V.tensor_tensor(parts[1], src, parts[0], ALU.subtract).then_inc(taken[kind], 1)
                elif kind == "vw":
                    b = c * 7
                    dve.wait_ge(high["vw"], count(c, label, kind, n))
                    if not (isinstance(c, int) and c == 0):
                        dve.wait_ge(v_step, b)
                    else:
                        dve.wait_ge(zeroed, 1)
                    rest = vrest.rearrange("p (w g d) -> p w g d", g=NG, d=DV)
                    part = [vwin[:, :, :, i * (DV + 1):i * (DV + 1) + DV] for i in range(3)]
                    V.tensor_tensor(rest, ps[:, :].rearrange("p (w g d) -> p w g d", g=NG, d=DV), part[0],
                                    ALU.subtract).then_inc(taken["vw"], 1)
                    dve.wait_ge(taken["vw"], count(c, label, kind, n))
                    V.tensor_copy(part[1], rest).then_inc(v_step, 1)
                    dve.wait_ge(v_step, b + 1)
                    V.tensor_tensor(part[2], rest, part[1], ALU.subtract).then_inc(v_step, 1)
                elif kind == "vf":
                    b = c * 7
                    dve.wait_ge(high["vf"], count(c, label, kind, n))
                    V.tensor_tensor(vfrest[:, :], ps[:, 0:64], vfp[:, 0, :], ALU.subtract).then_inc(taken["vf"], 1)
                    dve.wait_ge(taken["vf"], count(c, label, kind, n))
                    V.tensor_copy(vfp[:, 1, :], vfrest[:, :]).then_inc(v_step, 1)
                    dve.wait_ge(v_step, b + 3)
                    V.tensor_tensor(vfp[:, 2, :], vfrest[:, :], vfp[:, 1, :], ALU.subtract).then_inc(v_step, 1)
                    dve.wait_ge(v_step, b + 4)
                    half = half_of(c, label)
                    for t in range(4):
                        rows = slice(32 * t, 32 * t + 32)
                        if isinstance(c, int):
                            to = vdiag[rows, half, :, t * VP:(t + 1) * VP]
                        else:
                            to = vdiag[rows, bass.ds(half, 1), :, t * VP:(t + 1) * VP].rearrange("p a g n -> p (a g) n")
                        e = V.tensor_scalar(to.rearrange("p g (a n) -> p g a n", a=3)[:, :, :, 0:DV],
                                            vfp[rows, :, :].rearrange("p a (g d) -> p g a d", g=NG), 1.0, None, ALU.mult)
                    e.then_inc(v_step, 3)
                elif kind == "wo":
                    dve.wait_ge(done["wo"], count(c, label, kind, n))
                    ln_stats(1, [ps[:, i * D:(i + 1) * D] for i in range(2)], 2 * n, count(c, label, kind, n - 1) * LN)
                elif kind == "up":
                    dve.wait_ge(taken["up"], count(c, label, kind, n))
                    V.tensor_copy(x2_hl[0][:, 2 * (n % 4):2 * (n % 4) + 2, :],
                                  x2f[:, n % 2, :].rearrange("p (k n) -> p k n", k=2)).then_inc(x2h_done, 1)
                elif kind == "down":
                    dve.wait_ge(done["down"], count(c, label, kind, n))
                    f, i = divmod(n, 2)
                    if i == 0:
                        dve.wait_ge(stored[f], c * 16 + (16 * label + 16))
                    V.tensor_tensor(yo[:, n, :], ps[:, 0:D], bdn[:, :], ALU.add).then_inc(taken["down"], 1)
                    if i == 1:
                        dve.wait_ge(taken["down"], count(c, label, kind, n))
                        ln_stats(3, [yo[:, 2 * f + i, :] for i in range(2)], 2 * f, c * (2 * LN) + (2 * label + f) * LN)

            waiting = []

            def flush(c):
                if waiting:
                    rotate(c, *waiting.pop())

            def items(c, plans):
                for plan in plans:
                    label, (kind, n) = plan[0]
                    if kind == "vt":
                        flush(c)
                        continue
                    item(c, plan)
                    if kind == "rope":
                        flush(c)
                        waiting.append((label, n))

            def body_of(c, body):
                waiting[:] = [(NOW, ROPE_AT[("k", 1)])]
                slots, _ = planned(body)
                for n in range(SLOTS):
                    if body != FIRST or n >= 3:
                        sum_parts(c, n - 3, body)
                    maxima(c, n)
                    if body != FIRST or n:
                        prob_low(c, n - 1)
                    flush(c)
                    if body != FIRST or n >= 3:
                        normalise_heads(c, n - 3, body)
                    if n == 5 and body != FIRST:
                        stats_x1(c)
                    if n == 6 and body != FIRST:
                        norm_x1(c)
                    if n == 9 and body != FINAL:
                        norm_x(c, NEXT)
                    if body == FIRST and n == 4:
                        dequant(0)
                    if body == FIRST and n == 9:
                        dequant(1)
                    items(c, slots[n])
                    if n == 7 and body != FINAL:
                        stats_x(c, NEXT)
                if body == FIRST:
                    dve.wait_ge(done["wd"], 4)
                    dve.sem_inc(x1_free, 1)

            V.memset(vwin[:, :, :, :], 0.0).then_inc(fill_step, 1)
            dve.wait_ge(fill_step, 1)
            V.memset(vwin[:, :, :, DV:DV + 1], 1.0)
            V.memset(minus_half[:, :], -0.5)
            V.memset(vdiag[:, :, :, :], 0.0)
            V.memset(vt[:, 0:WIN], 0.0).then_inc(fill_step, 1)
            dve.wait_ge(fill_step, 2)
            for t in range(4):
                e = V.memset(vdiag[32 * t:32 * t + 32, :, :, t * VP + DV:t * VP + DV + 1], 1.0)
            e.then_inc(zeroed, 1)
            stats_x(-1, NEXT)
            norm_x(-1, NEXT)
            for name in ("wk", "wq0", "wv"):
                split_weight(name)
            items(-1, prologue)
            for name in WSEQ[3:]:
                split_weight(name)
            over_chunks(dve, body_of)
            sum_parts(NC - 1, SLOTS - 3, FINAL)
            prob_low(NC - 1, SLOTS - 1)
            sum_parts(NC - 1, SLOTS - 2, FINAL)
            sum_parts(NC - 1, SLOTS - 1, FINAL)
            normalise_heads(NC - 1, SLOTS - 1, FINAL)
            for plan in epilogue:
                item(NC, plan)
                if plan[0][1] == ("wo", 1):
                    stats_x1(NC)
                    norm_x1(NC)

        @block.gpsimd
        def _(pool):
            G = nc.gpsimd

            def item(c, plan):
                label, (kind, n) = plan[0]
                if kind == "rope":
                    pool.wait_ge(swapped, count(c, label, "rope", n))
                    if n == 0:
                        pool.wait_ge(ld_cs, c * 16 + 16 * (label + 1))
                    G.tensor_tensor(turned[:, n % 2, :], turned[:, n % 2, :], cs[:, 1, :], ALU.mult
                                    ).then_inc(sin_done, 1)
                elif kind == "up":
                    pool.wait_ge(x2h_done, count(c, label, kind, n))
                    k = 2 * (n % 4)
                    G.tensor_tensor(x2_hl[1][:, k:k + 2, :], x2f[:, n % 2, :].rearrange("p (k n) -> p k n", k=2),
                                    x2_hl[0][:, k:k + 2, :], ALU.subtract).then_inc(x2l_done, 1)
                elif kind == "down" and n % 2:
                    power(3, n - 1, 2, c * 2 + (2 * label + n // 2))
                elif kind == "wo":
                    power(1, 2 * n, 2, count(c, label, kind, n - 1))

            def residual(c, plan):
                label, (kind, n) = plan[0]
                if n == 0:
                    pool.wait_ge(ld_x1, c * 16 + 16 * (label + 1))
                pool.wait_ge(taken["wo"], count(c, label, kind, n))
                G.tensor_tensor(x1[:, 2 * n:2 * n + 2, :], x1[:, 2 * n:2 * n + 2, :], zn[:, 2 * n:2 * n + 2, :],
                                ALU.add).then_inc(x1_done, 1)

            def power(i, t0, n, before):
                pool.wait_ge(ln_step[i], before * LN + LN)
                G.tensor_tensor(rstd[:, i, t0:t0 + n], vareps[:, i, t0:t0 + n], minus_half[:, 0:n], ALU.pow
                                ).then_inc(rstd_done[i], 1)
                if i in shift_done:
                    pool.wait_ge(rstd_done[i], before + 1)
                    G.tensor_tensor(nmr[:, i, t0:t0 + n], minus_mean[:, i, t0:t0 + n], rstd[:, i, t0:t0 + n], ALU.mult
                                    ).then_inc(shift_done[i], 1)

            def power_x(c, label):
                power(0, 0, 4, c + label)

            def power_x1(c):
                for f in range(2):
                    power(2, 2 * f, 2, c * 2 + (2 * LAST + f))

            def gather_front(c, n):
                pool.wait_ge(exp_done, sets(c, n))
                if not (isinstance(c, int) and c == 0 and n == 0):
                    pool.wait_ge(t_done, sets(c, n - 1))
                pool.sem_inc(gates[pool.engine], 1)
                G.tensor_copy(pfront[:, :].rearrange("p (k n) -> p k n", k=4), prob[:, :, P:KEYS]
                              ).then_inc(pf_done, 1)

            def finish(c, label, n):
                pool.wait_ge(y_norm, c * 2 + (2 * label + n + 1))
                G.tensor_tensor(yo[:, 2 * n:2 * n + 2, :], yo[:, 2 * n:2 * n + 2, :], x1[:, 2 * n:2 * n + 2, :],
                                ALU.add).then_inc(x1_free, 1)

            def body_of(c, body):
                slots, _ = planned(body)
                for n in range(SLOTS):
                    gather_front(c, n)
                    if body == FIRST and n == 2:
                        pool.wait_ge(w_lo, len(WSEQ))
                        pool.wait_ge(v_step, 3)
                        G.memset(scratch[:, 2048:4608], 0.0).then_inc(padded, 1)
                    if n:
                        for (label, (kind, k)), _, _ in slots[n - 1]:
                            if kind == "down" and k % 2:
                                finish(c, label, k // 2)
                    if n == 5 and body != FIRST:
                        power_x1(c)
                    for plan in slots[n]:
                        item(c, plan)
                    if n == 7 and body != FINAL:
                        power_x(c, NEXT)
                    for plan in slots[n]:
                        if plan[0][1][0] == "wo":
                            residual(c, plan)

            pool.wait_ge(zeroed, 1)
            power_x(-1, NEXT)
            for plan in prologue:
                item(-1, plan)
            over_chunks(pool, body_of)
            for plan in epilogue:
                item(NC, plan)
                kind, n = plan[0][1]
                if kind == "wo":
                    residual(NC, plan)
                    if n == 1:
                        power_x1(NC)
                if kind == "down" and n % 2:
                    finish(NC, LAST, n // 2)


def constants():
    freq = (1.0 / THETA ** (np.arange(0, DQK, 2)[:DQK // 2].astype(np.float32) / DQK)).astype(np.float32)
    ang = np.outer(np.arange(S, dtype=np.float32), freq).T
    scale = np.float32(float(DQK) ** -0.25)
    cos, sin = np.cos(ang) * scale, np.sin(ang) * scale
    tables = np.stack([np.concatenate([cos, cos]), np.concatenate([-sin, sin])], 1)
    tables = tables.reshape(P, 2, HALVES, CH).transpose(2, 0, 1, 3)
    q = np.arange(P) % WIN
    half_masks = []
    for blk in range(3):
        row = WIN * blk + q[:, None]
        band_keys = WIN * (blk - 1) + np.arange(2 * WIN)[None, :]
        band = (band_keys >= 0) & (band_keys <= row) & (band_keys > row - WIN)
        front_keys = np.arange(FRONT)[None, :]
        front = front_keys <= row - WIN
        ok = np.concatenate([band, front], 1)
        half_masks.append(np.tile(np.where(ok, 0.0, MASKED), (1, 2)))
    mask01 = np.stack([np.stack([half_masks[0], half_masks[1]], 1), np.stack([half_masks[2]] * 2, 1)])
    return (np.ascontiguousarray(tables, dtype=np.float32), mask01, half_masks[2], np.eye(P))


_INS = ["L0_attn_x", "L0_attn_wq", "L0_attn_wk", "L0_attn_wv", "L0_attn_wo", "L0_ffn_w_up_q",
        "L0_ffn_w_up_scale", "L0_ffn_b_up", "L0_ffn_w_up_lora_a", "L0_ffn_w_up_lora_b", "L0_ffn_w_down_q",
        "L0_ffn_w_down_scale", "L0_ffn_b_down", "L0_ffn_w_down_lora_a", "L0_ffn_w_down_lora_b"]


def kernel(**inputs):
    import concourse.bacc as bacc
    from concourse.bass_utils import run_bass_kernel_spmd

    tables, mask01, mask2, eye = constants()
    bf16 = np.dtype("bfloat16")
    arrays = {name: np.ascontiguousarray(inputs[name]) for name in _INS}
    arrays |= {"tables": tables, "mask01": mask01.astype(bf16), "mask2": mask2.astype(bf16),
               "ident32": eye.astype(np.float32), "ident16": eye.astype(bf16)}
    nc = bacc.Bacc("TRN2", target_bir_lowering=False, num_devices=1)
    args = [nc.dram_tensor(f"in_{k}", a.shape, mybir.dt.from_np(a.dtype), kind="ExternalInput").ap()
            for k, a in arrays.items()]
    out = nc.dram_tensor("out", (B, S, D), F32, kind="ExternalOutput").ap()
    build(nc, *args, out)
    r = run_bass_kernel_spmd(nc, [{f"in_{k}": a for k, a in arrays.items()}], core_ids=[0])
    return r.results[0]["out"]
```

```python
from contextlib import ExitStack

import numpy as np

import concourse.bass as bass
from concourse import mybir

F32 = mybir.dt.float32
F32R = mybir.dt.float32r
F16 = mybir.dt.float16
BF16 = mybir.dt.bfloat16
I32 = mybir.dt.int32
ALU = mybir.AluOpType
ACT = mybir.ActivationFunctionType
AX_X = mybir.AxisListType.X

P = 128
B, S, D = 4, 1024, 256
NH, NG, DQK, DV = 16, 4, 128, 16
REP = NH // NG
WIN, FRONT = 64, 32
HID, RANK = 1024, 16
QBLK = 64
THETA = 10000.0
EPS = 1e-5
CH = 512
NC = B * S // CH
HALVES = S // CH
KC = D // P
HC = HID // P
BLK = CH // WIN
KEYS = 2 * WIN + FRONT
SLOTS = NG * BLK // 2
VP = 3 * (DV + 1)
PSCALE = 2.0 ** 14
MASKED = -1e30
ROPES = NG * (REP + 1)

PER_CHUNK = {"rope": ROPES, "vt": 1, "vw": 1, "vf": 1, "ot": 2, "wo": 2, "xa": 2, "up": 8,
             "down": 4, "xn": 2, "wt": 3, "wu": 4, "wd": 4}


def rope(*tile):
    return ("rope", tile)


NOW, NEXT, LAST, SETUP = 0, 1, -1, "setup"
JOBS = {
    0: [(NOW, rope("q", 1, 1)), (NOW, rope("q", 1, 2))],
    1: [(NOW, rope("q", 1, 3)), (NOW, ("vw", 0)), (NOW, ("vf", 0))],
    2: [(NOW, rope("q", 2, 0)), (NOW, rope("q", 2, 1))],
    3: [(LAST, ("ot", 0)), (LAST, ("ot", 1)), (NOW, rope("q", 2, 2))],
    4: [(LAST, ("wo", 0)), (LAST, ("wo", 1)), (NOW, rope("k", 2))],
    5: [(NOW, rope("q", 2, 3))],
    6: [(NOW, rope("q", 3, 0)), (NOW, rope("q", 3, 1))],
    7: [(NOW, rope("k", 3)), (LAST, ("xa", 0)), (LAST, ("xa", 1))],
    8: [(LAST, ("up", 0)), (LAST, ("up", 1)), (NOW, rope("q", 3, 2))],
    9: [(LAST, ("up", 2)), (LAST, ("up", 3)), (NOW, rope("q", 3, 3))],
    10: [(NEXT, ("xn", 0)), (NEXT, ("xn", 1)), (LAST, ("down", 0))],
    11: [(NEXT, rope("k", 0)), (LAST, ("down", 1)), (NEXT, rope("q", 0, 0))],
    12: [(LAST, ("up", 4)), (LAST, ("up", 5)), (NEXT, rope("q", 0, 1))],
    13: [(LAST, ("up", 6)), (LAST, ("up", 7)), (NEXT, rope("q", 0, 2))],
    14: [(LAST, ("down", 2)), (LAST, ("down", 3)), (NEXT, rope("q", 0, 3))],
    15: [(NEXT, rope("k", 1)), (NEXT, ("vt", 0)), (NEXT, rope("q", 1, 0))],
}
ROPE_ORDER = [job[1] for wanted in (NEXT, NOW) for n in range(SLOTS) for label, job in JOBS[n]
              if label == wanted and job[0] == "rope"]
ROPE_AT = {tile: n for n, tile in enumerate(ROPE_ORDER)}
JOBS = {n: [(label, (kind, ROPE_AT[k] if kind == "rope" else k)) for label, (kind, k) in jobs]
        for n, jobs in JOBS.items()}
ON_POOL = [ROPE_AT[tile] for tile in [("q", 2, h) for h in range(REP)] + [("q", 3, 0), ("q", 3, 1)]]
SETUP_JOBS = {3: [("wt", 0), ("wt", 1), ("wt", 2)], 5: [("wu", 0)], 6: [("wu", 1)], 7: [("wu", 2)],
              8: [("wu", 3)], 10: [("wd", 0)], 11: [("wd", 1)], 12: [("wd", 2)], 13: [("wd", 3)]}
PROLOGUE = [job for n in range(SLOTS) for job in JOBS[n] if job[0] == NEXT]
EPILOGUE = [(LAST, (kind, n)) for kind, n in [("ot", 0), ("ot", 1), ("wo", 0), ("wo", 1), ("xa", 0), ("xa", 1)]
            + [("up", n) for n in range(4)] + [("down", 0), ("down", 1)]
            + [("up", n) for n in range(4, 8)] + [("down", 2), ("down", 3)]]
BANKS = 4
LN = 3
FIRST, MIDDLE, FINAL = "first", "middle", "final"


def jobs_of(body, slot):
    found = [j for j in JOBS[slot] if not (body == FIRST and j[0] == LAST)
             and not (body == FINAL and j[0] == NEXT)]
    if body == FIRST:
        found = [(SETUP, j) for j in SETUP_JOBS.get(slot, [])] + found
    return found


def plan_banks(jobs, before):
    n, plan = len(jobs), []
    held = dict(enumerate(before))
    for i, job in enumerate(jobs):
        bank = (i - n) % BANKS
        plan.append((job, bank, held.get(bank)))
        held[bank] = job
    return plan, [held[b] for b in range(BANKS)]


def older(jobs):
    return [(label if label == SETUP else label - 1, job) for label, job in jobs]


def build(nc, x, wq, wk, wv, wo, up_q, up_scale, b_up, up_a, up_b, down_q, down_scale, b_down,
          down_a, down_b, tables, mask01, mask2, ident32, ident16, out):
    ctx = ExitStack()
    with ctx:
        def sb(name, shape, dt=F32):
            return ctx.enter_context(nc.sbuf_tensor(name, shape, dt))

        def sem(name):
            return ctx.enter_context(nc.semaphore(name))

        wq_hl = [sb(f"wq_{p}", [P, KC, NH * DQK], F32R) for p in "hl"]
        wk_hl = [sb(f"wk_{p}", [P, KC, NG * DQK], F32R) for p in "hl"]
        wv_hl = [sb(f"wv_{p}", [P, KC, NG * DV], F32R) for p in "hl"]
        wo_hl = [sb(f"wo_{p}", [P, 2, D], F32R) for p in "hl"]
        wup_hl = [sb(f"wup_{p}", [P, KC, HID], F32R) for p in "hl"]
        wdn_hl = [sb(f"wdn_{p}", [P, HC, D], F32R) for p in "hl"]
        id32 = sb("id32", [P, P])
        id16 = sb("id16", [P, P], BF16)
        bup = sb("bup", [P, HC])
        bdn = sb("bdn", [P, D])
        scu = sb("scu", [P, HC, D // QBLK])
        scd = sb("scd", [P, KC, HID // QBLK])
        cs = sb("cs", [P, 2, CH])
        m01 = sb("m01", [P, 2, 2 * KEYS], BF16)
        m2 = sb("m2", [P, 2 * KEYS], BF16)
        xa = sb("xa", [P, 4, D])
        xt_hl = [sb(f"xt_{p}", [P, KC, CH], F32R) for p in "hl"]
        turned = sb("turned", [P, 2, CH])
        straight = sb("straight", [P, 2, CH])
        qrot = sb("qrot", [P, 2, BLK, REP, WIN])
        kwin = sb("kwin", [P, NG, BLK, KEYS])
        kfront = sb("kfront", [P, FRONT])
        vt = sb("vt", [4 * DV, WIN + CH])
        vtf = sb("vtf", [4 * DV, 4 * FRONT])
        vwin = sb("vwin", [P, BLK, NG, VP], BF16)
        vfrest = sb("vfrest", [P, 4 * DV])
        vfp = sb("vfp", [P, 3, 4 * DV], BF16)
        vdiag = sb("vdiag", [P, 2, NG, 4 * VP], BF16)
        nmax = sb("nmax", [P, 2, 4])
        prob = sb("prob", [P, 4, KEYS])
        pfront = sb("pfront", [P, 4 * FRONT])
        p_hl = [sb(f"p_{p}", [P, 2, 5 * P], F16) for p in "hl"]
        osum = sb("osum", [P, 4, 4, DV + 1])
        rsum = sb("rsum", [P, 16])
        oall = sb("oall", [P, BLK, P])
        ot_hl = [sb(f"ot_{p}", [P, 2, CH], F32R) for p in "hl"]
        x2_hl = [sb(f"x2_{p}", [P, HC, CH // 2], F32R) for p in "hl"]
        scratch = sb("scratch", [P, 4608])
        zn = scratch[:, 0:1024].rearrange("p (t d) -> p t d", t=4)
        x1 = scratch[:, 1024:2048].rearrange("p (t d) -> p t d", t=4)
        yo = scratch[:, 2048:3072].rearrange("p (t d) -> p t d", t=4)
        x2f = scratch[:, 3072:4096].rearrange("p (b n) -> p b n", b=2)
        vrest = scratch[:, 4096:4608]
        wq_st = scratch[:, 0:2048].rearrange("p (b k n) -> p b k n", b=2, k=KC)
        wk_st = scratch[:, 2048:3072].rearrange("p (k n) -> p k n", k=KC)
        wv_st = scratch[:, 3072:3200].rearrange("p (k n) -> p k n", k=KC)
        wo_st = scratch[:, 3200:3712].rearrange("p (k n) -> p k n", k=2)
        deq = scratch[:, 0:2048]
        upb_st = scratch[:, 2048:3072]
        dnb_st = scratch[:, 3072:3328]
        upa_t = scratch[:, 3328:3584]
        dna_t = scratch[:, 3584:4608]
        upa_st = sb("upa_st", [P, KC, RANK])
        dna_st = sb("dna_st", [P, HC, RANK])
        st = sb("st", [P, 4, 4, 6])
        mv = sb("mv", [P, 4, 4, 2])
        vareps = sb("vareps", [P, 4, 4])
        rstd = sb("rstd", [P, 4, 4])
        minus_half = sb("minus_half", [P, 4])
        minus_mean = sb("minus_mean", [P, 4, 4])
        nmr = sb("nmr", [P, 4, 4])

        ring = [ctx.enter_context(nc.psum_tensor(f"ring{b}", [P, CH], F32)) for b in range(BANKS)]
        ps_s = ctx.enter_context(nc.psum_tensor("ps_s", [P, 2, 512], F32))
        ps_t = ctx.enter_context(nc.psum_tensor("ps_t", [P, 1024], F32))
        ps_v = ps_t[:, 5 * P:5 * P + 4 * VP]

        done = {k: sem(f"{k}_done") for k in PER_CHUNK}
        high = {k: sem(f"{k}_high") for k in ("xn", "ot", "xa", "wu", "wd", "vw", "vf")}
        taken = {k: sem(f"{k}_taken") for k in PER_CHUNK}
        swapped = sem("halves_swapped")
        sin_done = sem("sines_applied")
        rot_done = sem("tiles_rotated")
        k_step = sem("key_steps")
        s_done = sem("scores_done")
        max_done = sem("maxima_done")
        exp_done = sem("exp_done")
        pf_done = sem("front_probs_gathered")
        t_done = sem("prob_transposed")
        ph_done = sem("prob_high_done")
        pl_done = sem("prob_low_done")
        pv_done = sem("pv_done")
        os_done = sem("pv_summed")
        r_done = sem("sums_inverted")
        o_done = sem("heads_normalised")
        v_carry = sem("value_carried")
        v_wide = sem("value_window_parts")
        v_step = sem("front_value_parts")
        ln_step = [sem(f"ln{i}_steps") for i in range(4)]
        rstd_done = [sem(f"ln{i}_rstd") for i in range(4)]
        shift_done = [sem(f"ln{i}_shift") for i in range(4)]
        xn_done = sem("x_normalised")
        z_done = sem("attention_normalised")
        x1_done = sem("x1_done")
        x1n_done = sem("x1_normalised")
        x2h_done = sem("hidden_high_done")
        x2l_done = sem("hidden_low_done")
        y_norm = sem("network_normalised")
        x1_free = sem("x1_free")
        stored = [sem(f"stored{i}") for i in range(2)]
        ld_x = sem("x_loaded")
        ld_x1 = sem("x_reloaded")
        ld_cs = sem("tables_loaded")
        ld_m = sem("masks_loaded")
        ld_w = {k: sem(f"{k}_loaded") for k in ("wk", "wq0", "wq1", "wq2", "wq3", "wv", "wo", "ident",
                                                 "small", "upq", "downq", "rank")}
        w_hi = sem("weights_high")
        w_lo = sem("weights_low")
        fill_step = sem("fill_steps")
        gates = {e.engine: sem(f"gate{i}") for i, e in enumerate((nc.tensor, nc.vector, nc.gpsimd))}
        zeroed = sem("zeroed")
        padded = sem("factors_zeroed")
        deq_done = sem("dequantised")
        WSEQ = ["wk", "wq0", "wv", "wq1", "wq2", "wq3", "wo"]

        x_v = x.rearrange("b (c t p) d -> (b c) p t d", p=P, t=4)
        out_v = out.rearrange("b (c f t p) d -> (b c) f p t d", p=P, f=2, t=2)

        def count(c, label, kind, n):
            if label == SETUP:
                return n + 1
            per = PER_CHUNK[kind]
            return c * per + (label * per + n + 1)

        def half_of(c, label):
            return (c + label) % HALVES

        def sets(c, n):
            return c * SLOTS + (n + 1)

        def over_chunks(e, body_of):
            body_of(0, FIRST)
            with e.Fori(1, NC - 1) as c:
                body_of(c, MIDDLE)
            body_of(NC - 1, FINAL)

        def planned(body):
            jobs = [j for n in range(SLOTS) for j in jobs_of(body, n)]
            plan, tail = plan_banks(jobs, older(PROLOGUE[-BANKS:]))
            by_slot, at = [], 0
            for n in range(SLOTS):
                k = len(jobs_of(body, n))
                by_slot.append(plan[at:at + k])
                at += k
            return by_slot, tail

        prologue = plan_banks(PROLOGUE, [None] * BANKS)[0]
        tail = planned(FINAL)[1]
        epilogue = plan_banks(EPILOGUE, older(tail))[0]

        def values_after(n, jobs):
            if n == 1:
                return 1
            work = sum({"ot": 1, "xa": 1, "xn": 1, "down": 6}.get(plan[0][1][0], 3) for plan in jobs[:-1])
            return len(jobs) - 1 if work >= 6 else len(jobs)

        def held(e, q, value):
            e.wait_ge(q, value)
            e.sem_inc(gates[e.engine], 1)

        block = ctx.enter_context(nc.Block())

        @block.sync
        def _(sp):
            def load_x(c, waited):
                if waited:
                    sp.wait_ge(done["xn"], count(c, NOW, "xn", 1))
                    sp.dma_start(xa[:, :, :], x_v[bass.ds(c + 1, 1)].rearrange("a p t d -> p (a t) d")).then_inc(ld_x, 16)
                else:
                    sp.dma_start(xa[:, :, :], x_v[0]).then_inc(ld_x, 16)

            def load_tables(c, label):
                src = tables[bass.ds(half_of(c, label), 1)] if not isinstance(c, int) else \
                    tables[half_of(c, label):half_of(c, label) + 1]
                sp.dma_start(cs[:, :, :], src.rearrange("a p t n -> p (a t) n")).then_inc(ld_cs, 16)

            def load_masks(c, label):
                src = mask01[bass.ds(half_of(c, label), 1)] if not isinstance(c, int) else \
                    mask01[half_of(c, label):half_of(c, label) + 1]
                sp.dma_start(m01[:, :, :], src.rearrange("a p t n -> p (a t) n")).then_inc(ld_m, 16)

            def load_wq(g):
                if g >= 2:
                    sp.wait_ge(w_lo, WSEQ.index(f"wq{g - 2}") + 1)
                sp.dma_start(wq_st[:, g % 2, :, :],
                             wq.rearrange("(k p) n -> p k n", p=P)[:, :, g * 512:(g + 1) * 512]
                             ).then_inc(ld_w[f"wq{g}"], 16)

            def store(c, f):
                sp.wait_ge(x1_free, c * 2 + (f - 2 + 2))
                at = out_v[bass.ds(c - 1, 1), f].rearrange("a p t d -> p (a t) d")
                sp.dma_start(at, yo[:, 2 * f:2 * f + 2, :]).then_inc(stored[f], 16)

            def setup_loads():
                for q in stored:
                    sp.sem_inc(q, 16)
                load_x(0, False)
                sp.dma_start(id32[:, :], ident32).then_inc(ld_w["ident"], 16)
                sp.dma_start(id16[:, :], ident16).then_inc(ld_w["ident"], 16)
                sp.dma_start(wk_st, wk.rearrange("(k p) n -> p k n", p=P)).then_inc(ld_w["wk"], 16)
                load_wq(0)
                load_tables(0, NOW)
                sp.dma_start(wv_st, wv.rearrange("(k p) n -> p k n", p=P)).then_inc(ld_w["wv"], 16)
                load_masks(0, NOW)
                sp.dma_start(m2[:, :], mask2).then_inc(ld_w["ident"], 16)
                load_wq(1)
                for hh in range(2):
                    sp.dma_start(wo_st[:, hh, :], wo.rearrange("(a hh d) n -> hh a d n", hh=2, d=DV)[hh]
                                 ).then_inc(ld_w["wo"], 16)
                sp.dma_start(bup[:, :], b_up.rearrange("(k p) -> p k", p=P), allow_slow_non_contiguous=True
                             ).then_inc(ld_w["small"], 16)
                sp.dma_start(bdn[:, :], b_down.rearrange("(a n) -> a n", a=1).broadcast_to([P, D])).then_inc(ld_w["small"], 16)
                sp.dma_start(scu[:, :, :], up_scale.rearrange("(k p) n -> p k n", p=P)).then_inc(ld_w["small"], 16)
                sp.dma_start(scd[:, :, :], down_scale.rearrange("(k p) n -> p k n", p=P)).then_inc(ld_w["small"], 16)
                sp.dma_start(upa_st[:, :, :], up_a.rearrange("(k p) n -> p k n", p=P)).then_inc(ld_w["small"], 16)
                sp.dma_start(dna_st[:, :, :], down_a.rearrange("(k p) n -> p k n", p=P)).then_inc(ld_w["small"], 16)
                load_wq(2)
                load_wq(3)

            def setup_loads_late():
                sp.wait_ge(w_lo, len(WSEQ))
                sp.dma_start(deq.bitcast(I32).rearrange("p (k n) -> p k n", k=HC),
                             up_q.rearrange("(k p) n -> p k n", p=P)).then_inc(ld_w["upq"], 16)
                sp.wait_ge(padded, 1)
                sp.dma_start(upb_st[0:RANK, :], up_b).then_inc(ld_w["rank"], 16)
                sp.dma_start(dnb_st[0:RANK, :], down_b).then_inc(ld_w["rank"], 16)

            def setup_loads_last():
                sp.wait_ge(done["wu"], 4)
                sp.dma_start(deq.bitcast(I32).rearrange("p (k n) -> p k n", k=KC),
                             down_q.rearrange("(k p) n -> p k n", p=P)).then_inc(ld_w["downq"], 16)

            def body_of(c, body):
                if body != FINAL:
                    load_x(c, True)
                if body == FIRST:
                    setup_loads_late()
                    setup_loads_last()
                else:
                    sp.wait_ge(x1_free, c * 2 - 1)
                    sp.dma_start(x1, x_v[bass.ds(c - 1, 1)].rearrange("a p t d -> p (a t) d")
                                 ).then_inc(ld_x1, 16)
                if body != FINAL:
                    sp.wait_ge(taken["rope"], count(c, NOW, "rope", ROPES - 1))
                    sp.wait_ge(sin_done, count(c, NOW, "rope", ROPES - 1))
                    load_tables(c, NEXT)
                if body != FIRST:
                    store(c, 0)
                if body != FINAL:
                    sp.wait_ge(s_done, sets(c, SLOTS - 4))
                    load_masks(c, NEXT)
                if body != FIRST:
                    store(c, 1)

            setup_loads()
            over_chunks(sp, body_of)
            sp.wait_ge(x1_free, NC * 2 - 1)
            sp.dma_start(x1, x_v[NC - 1]).then_inc(ld_x1, 16)
            store(NC, 0)
            store(NC, 1)
            for q in stored:
                sp.wait_ge(q, 16 * (NC + 1))

        @block.tensor
        def _(pe):
            PASSES = ((0, 0), (0, 1), (1, 0))

            def claim(c, before):
                if before is not None:
                    label, (kind, n) = before
                    held(pe, taken[kind], count(c, label, kind, n))

            def scores(c, n, body):
                g, s = divmod(n, NG)
                if s == 0:
                    pe.wait_ge(k_step, c * (4 * NG) + 4 * g + 4)
                    pe.wait_ge(rot_done, count(c, NOW, "rope", ROPE_AT[("q", g, REP - 1)]))
                if n == 0:
                    pe.wait_ge(ld_m, c * 16 + 16)
                if body != FIRST or n:
                    pe.wait_ge(exp_done, sets(c, n - 1))
                for bb in range(2):
                    blk = 2 * s + bb
                    mask = m01[:, bb, :] if s == 0 else m2[:, :]
                    pe.matmul(ps_s[:, bb, 0:2 * KEYS], id16[:, :], mask, start=True, stop=False,
                              skip_group_check=True)
                    for pr in range(2):
                        mm = pe.matmul(ps_s[:, bb, pr * KEYS:(pr + 1) * KEYS],
                                       qrot[:, g % 2, blk, 2 * pr:2 * pr + 2, :].rearrange("p r q -> p (r q)"),
                                       kwin[:, g, blk, :],
                                       start=False, stop=True, skip_group_check=True)
                mm.then_inc(s_done, 1)

            def transposes(c, m, body):
                pe.wait_ge(exp_done, sets(c, m))
                if body != FIRST or m:
                    pe.wait_ge(pl_done, sets(c, m - 1))
                for k in range(4):
                    pe.transpose(ps_t[:, k * P:(k + 1) * P], prob[:, k, 0:P], id32[:, :])
                pe.wait_ge(pf_done, sets(c, m))
                if body != FIRST or m >= 2:
                    pe.wait_ge(os_done, sets(c, m - 2))
                pe.transpose(ps_t[:, 4 * P:5 * P], pfront[:, :], id32[:, :]).then_inc(t_done, 1)

            def values(c, m, body):
                g, s = divmod(m % SLOTS, NG)
                last = body == FINAL and m == SLOTS - 1
                pe.wait_ge(pl_done, sets(c, m if last else m + 1))
                if last:
                    pe.wait_ge(os_done, sets(c, m - 1))
                if m == 0:
                    pe.wait_ge(v_wide, c * 2 + 2)
                    pe.wait_ge(v_step, c * 5 + 5)
                lo = 2 * (DV + 1)
                ph, pl = (t[:, m % 2, :] for t in p_hl)
                diag = vdiag[:, 0, g, :]
                pe.matmul(ps_v, ph[:, 4 * P:5 * P], diag, start=True, stop=False,
                          skip_group_check=True)
                pe.matmul(ps_v.rearrange("p (k n) -> p k n", n=VP)[:, :, 0:lo], pl[:, 4 * P:5 * P],
                          diag.rearrange("p (k n) -> p k n", n=VP)[:, :, 0:lo], start=False, stop=False,
                          skip_group_check=True)
                for k in range(4):
                    w = vwin[:, 2 * s + k // 2, g, :]
                    pe.matmul(ps_v[:, k * VP:(k + 1) * VP], ph[:, k * P:(k + 1) * P], w,
                              start=False, stop=False, skip_group_check=True)
                    mm = pe.matmul(ps_v[:, k * VP:k * VP + lo], pl[:, k * P:(k + 1) * P], w[:, 0:lo],
                                   start=False, stop=True, skip_group_check=True)
                mm.then_inc(pv_done, 1)

            def three_passes(to, terms, start=True):
                for i, (a, b) in enumerate(terms):
                    for j, (pa, pb) in enumerate(PASSES):
                        mm = pe.matmul(to, a[pa], b[pb], start=start and i == 0 and j == 0,
                                       stop=i == len(terms) - 1 and j == len(PASSES) - 1)
                return mm

            def job(c, plan):
                (label, (kind, n)), bank, before = plan
                claim(c, before)
                to = ring[bank]
                if kind == "rope":
                    tile = ROPE_ORDER[n]
                    if n == 0:
                        pe.wait_ge(taken["xn"], count(c, label, "xn", KC - 1))
                    if isinstance(c, int) and c + label == 0:
                        name = "wk" if tile[0] == "k" else f"wq{tile[1]}"
                        pe.wait_ge(w_lo, WSEQ.index(name) + 1)
                    if tile[0] == "k":
                        w, at = wk_hl, tile[1] * DQK
                    else:
                        w, at = wq_hl, (tile[1] * REP + tile[2]) * DQK
                    mm = three_passes(to[:, :], [([t[:, k, at:at + DQK] for t in w], [t[:, k, :] for t in xt_hl])
                                                 for k in range(KC)])
                elif kind == "xn":
                    pe.wait_ge(xn_done, c * 1 + (label + 1))
                    if isinstance(c, int) and c < 0:
                        pe.wait_ge(ld_w["ident"], 48)
                    for t in range(4):
                        mm = pe.transpose(to[:, t * P:(t + 1) * P], xa[:, t, n * P:(n + 1) * P], id32[:, :])
                elif kind == "vt":
                    if isinstance(c, int) and c < 0:
                        pe.wait_ge(w_lo, WSEQ.index("wv") + 1)
                    mm = three_passes(to[0:NG * DV, :], [([t[:, k, :] for t in wv_hl], [t[:, k, :] for t in xt_hl])
                                                         for k in range(KC)])
                elif kind == "vw":
                    held(pe, taken["vt"], count(c, label, "vt", 0))
                    for w in range(BLK):
                        mm = pe.transpose(to[:, w * 64:(w + 1) * 64], vt[:, w * WIN:(w + 2) * WIN],
                                          id32[0:64, 0:64])
                elif kind == "vf":
                    mm = pe.transpose(to[:, 0:64], vtf[:, :], id32[0:64, 0:64])
                elif kind == "ot":
                    pe.wait_ge(o_done, c * NG + (label + 1) * NG)
                    for b in range(4):
                        mm = pe.transpose(to[:, b * P:(b + 1) * P], oall[:, 4 * n + b, :], id32[:, :])
                elif kind == "wo":
                    if n == 0:
                        pe.wait_ge(taken["ot"], count(c, label, "ot", 1))
                    for i in range(2):
                        t = 2 * n + i
                        mm = three_passes(to[:, i * D:(i + 1) * D],
                                          [([o[:, hh, t * P:(t + 1) * P] for o in ot_hl], [w[:, hh, :] for w in wo_hl])
                                           for hh in range(2)])
                elif kind == "xa":
                    pe.wait_ge(x1n_done, c * 2 + (2 * label + 2))
                    for t in range(4):
                        mm = pe.transpose(to[:, t * P:(t + 1) * P], zn[:, t, n * P:(n + 1) * P], id32[:, :])
                elif kind == "up":
                    if n == 0:
                        pe.wait_ge(taken["xa"], count(c, label, "xa", 1))
                    f, h0 = n // 4, 2 * (n % 4)
                    for i in range(2):
                        at = (h0 + i) * P
                        mm = three_passes(to[:, i * 256:(i + 1) * 256],
                                          [([w[:, k, at:at + P] for w in wup_hl],
                                            [o[:, k, f * 256:(f + 1) * 256] for o in ot_hl]) for k in range(KC)])
                elif kind == "down":
                    pe.wait_ge(x2l_done, count(c, label, "up", 4 * (n // 2) + 3))
                    i = n % 2
                    mm = three_passes(to[:, 0:D], [([o[:, k, i * P:(i + 1) * P] for o in x2_hl],
                                                    [w[:, k, :] for w in wdn_hl]) for k in range(HC)])
                elif kind == "wt":
                    pe.wait_ge(ld_w["small"], 96)
                    blocks = [upa_st[:, k, :] for k in range(KC)] if n == 0 else \
                        [dna_st[:, 4 * (n - 1) + k, :] for k in range(4)]
                    for i, a in enumerate(blocks):
                        mm = pe.transpose(to[0:RANK, i * P:(i + 1) * P], a, id32[:, :])
                elif kind == "wu":
                    if n == 0:
                        pe.wait_ge(taken["wt"], 3)
                        pe.wait_ge(ld_w["rank"], 32)
                        pe.wait_ge(deq_done, 1)
                    k, hh = n // 2, n % 2
                    pe.matmul(to[:, :], upa_t[:, k * P:(k + 1) * P], upb_st[:, hh * 512:(hh + 1) * 512],
                              start=True, stop=False, skip_group_check=True)
                    for i in range(4):
                        t = deq.rearrange("p (k n) -> p k n", k=HC)[:, 4 * hh + i, k * P:(k + 1) * P]
                        mm = pe.matmul(to[:, i * P:(i + 1) * P], t, id32[:, :], start=False, stop=True,
                                       skip_group_check=True)
                elif kind == "wd":
                    if n == 0:
                        pe.wait_ge(deq_done, 2)
                    for i in range(2):
                        h = 2 * n + i
                        pe.matmul(to[:, i * D:(i + 1) * D], dna_t[:, h * P:(h + 1) * P], dnb_st[:, :],
                                  start=i == 0, stop=False, skip_group_check=True)
                        for o in range(KC):
                            t = deq.rearrange("p (k n) -> p k n", k=KC)[:, o, h * P:(h + 1) * P]
                            mm = pe.matmul(to[:, i * D + o * P:i * D + (o + 1) * P], t, id32[:, :],
                                           start=False, stop=True, skip_group_check=True)
                mm.then_inc(done[kind], 1)

            def body_of(c, body):
                slots, _ = planned(body)
                for n in range(SLOTS):
                    scores(c, n, body)
                    if body != FIRST or n >= 1:
                        transposes(c, n - 1, body)
                    jobs = slots[n]
                    at = values_after(n, jobs)
                    for plan in jobs[:at]:
                        job(c, plan)
                    if body != FIRST or n >= 2:
                        values(c, n - 2, body)
                    for plan in jobs[at:]:
                        job(c, plan)

            for plan in prologue:
                job(-1, plan)
            over_chunks(pe, body_of)
            transposes(NC - 1, SLOTS - 1, FINAL)
            values(NC - 1, SLOTS - 2, FINAL)
            values(NC - 1, SLOTS - 1, FINAL)
            for plan in epilogue:
                job(NC, plan)

        def hi_lo(kind, n, bank):
            to = ring[bank][:, :]
            if kind == "xn":
                return [t[:, n, :] for t in xt_hl], to
            if kind == "xa":
                return [t[:, n, :] for t in ot_hl], to
            if kind == "ot":
                return [t[:, :, n * 256:(n + 1) * 256].rearrange("p h (b q) -> p b h q", q=WIN) for t in ot_hl], \
                    to.rearrange("p (b h q) -> p b h q", b=4, h=2)
            if kind == "wu":
                return [t[:, n // 2, (n % 2) * 512:(n % 2 + 1) * 512] for t in wup_hl], to
            return [t[:, 2 * n:2 * n + 2, :] for t in wdn_hl], to.rearrange("p (k n) -> p k n", k=2)

        def value_parts():
            return vrest.rearrange("p (w g d) -> p w g d", g=NG, d=DV), \
                [vwin[:, :, :, i * (DV + 1):i * (DV + 1) + DV] for i in range(3)]

        def rotated_queries(n):
            _, g, h = ROPE_ORDER[n]
            return [qrot[:, g % 2, :, h, :]] + [t[:, n % 2, :].rearrange("p (b n) -> p b n", n=WIN)
                                                for t in (straight, turned)]

        def weight(name):
            if name[:2] == "wv":
                return [(wv_st[:, k, :], [t[:, k, :] for t in wv_hl]) for k in range(KC)]
            if name[:2] == "wo":
                return [(wo_st[:, k, :], [t[:, k, :] for t in wo_hl]) for k in range(2)]
            if name[:2] == "wk":
                src, parts, at = wk_st, wk_hl, 0
            else:
                g = int(name[2])
                src, parts, at = wq_st[:, g % 2, :, :], wq_hl, g * 512
            return [(src[:, k, :].rearrange("p (h f t) -> p h t f", h=4, t=2),
                     [t[:, k, at:at + 512].rearrange("p (h t f) -> p h t f", h=4, t=2) for t in parts])
                    for k in range(KC)]

        @block.scalar
        def _(act):
            def exp(c, n):
                act.wait_ge(max_done, sets(c, n))
                if not (isinstance(c, int) and c == 0 and n == 0):
                    act.wait_ge(t_done, sets(c, n - 1))
                for k in range(4):
                    e = nc.scalar.activation(prob[:, k, :],
                                             ps_s[:, k // 2, (k % 2) * KEYS:(k % 2 + 1) * KEYS],
                                             ACT.Exp, bias=nmax[:, n % 2, k:k + 1])
                e.then_inc(exp_done, 1)

            def prob_high(c, m):
                act.wait_ge(t_done, sets(c, m))
                nc.scalar.activation(p_hl[0][:, m % 2, :], ps_t[:, 0:5 * P], ACT.Copy, scale=PSCALE
                                     ).then_inc(ph_done, 1)

            def split_weight(name):
                i = WSEQ.index(name)
                act.wait_ge(ld_w[name], 32 if name == "wo" else 16)
                for src, parts in weight(name):
                    e = nc.scalar.activation(parts[0], src, ACT.Copy)
                e.then_inc(w_hi, 1)

            def item(c, plan):
                (label, (kind, n)), bank, _ = plan
                ps = ring[bank]
                act.wait_ge(done[kind], count(c, label, kind, n))
                if kind == "rope":
                    if not (isinstance(c, int) and c + label == 0 and n < 2):
                        act.wait_ge(rot_done, count(c, label, kind, n - 2))
                    nc.scalar.activation(turned[0:64, n % 2, :], ps[64:128, :], ACT.Copy)
                    nc.scalar.activation(turned[64:128, n % 2, :], ps[0:64, :], ACT.Copy).then_inc(swapped, 1)
                elif kind == "vt":
                    if isinstance(c, int) and c < 0:
                        act.wait_ge(zeroed, 1)
                    else:
                        nc.scalar.activation(vt[:, 0:WIN], vt[:, CH:CH + WIN], ACT.Copy).then_inc(v_carry, 1)
                        act.wait_ge(v_carry, c + (label + 0))
                    nc.scalar.activation(vtf[:, :].rearrange("p (k n) -> p k n", k=4),
                                         ps[0:64, 0:FRONT].unsqueeze(1).broadcast_to([64, 4, FRONT]), ACT.Copy)
                    nc.scalar.activation(vt[:, WIN:], ps[0:64, :], ACT.Copy).then_inc(taken["vt"], 1)
                elif kind == "vw":
                    nc.scalar.activation(vwin[:, :, :, 0:DV], ps[:, :].rearrange("p (w g d) -> p w g d", g=NG, d=DV),
                                         ACT.Copy).then_inc(high["vw"], 1)
                elif kind == "vf":
                    nc.scalar.activation(vfp[:, 0, :], ps[:, 0:64], ACT.Copy).then_inc(high["vf"], 1)
                elif kind == "wo":
                    act.wait_ge(shift_done[1], count(c, label, "wo", n))
                    for i in range(2):
                        e = normalise(1, zn[:, 2 * n + i, :], ps[:, i * D:(i + 1) * D], 2 * n + i)
                    e.then_inc(taken["wo"], 1)
                elif kind == "up":
                    if n >= 2:
                        act.wait_ge(x2l_done, count(c, label, kind, n - 2))
                    for i in range(2):
                        h = 2 * (n % 4) + i
                        e = nc.scalar.activation(x2f[:, n % 2, i * 256:(i + 1) * 256], ps[:, i * 256:(i + 1) * 256],
                                                 ACT.Relu, bias=bup[:, h:h + 1])
                    e.then_inc(taken["up"], 1)
                elif kind == "wt":
                    act.wait_ge(padded, 1)
                    if n == 0:
                        nc.scalar.activation(upa_t[0:RANK, :], ps[0:RANK, 0:256], ACT.Copy).then_inc(taken["wt"], 1)
                    else:
                        nc.scalar.activation(dna_t[0:RANK, (n - 1) * 512:n * 512], ps[0:RANK, :], ACT.Copy
                                             ).then_inc(taken["wt"], 1)
                else:
                    parts, src = hi_lo(kind, n, bank)
                    nc.scalar.activation(parts[0], src, ACT.Copy).then_inc(high[kind], 1)

            def normalise(i, to, src, t):
                return nc.scalar.activation(to, src, ACT.Identity, bias=nmr[:, i, t:t + 1], scale=rstd[:, i, t:t + 1])

            def normalise_x1(c):
                for f in range(2):
                    act.wait_ge(shift_done[2], c * 2 + (2 * LAST + f + 1))
                    for t in (2 * f, 2 * f + 1):
                        e = normalise(2, zn[:, t, :], x1[:, t, :], t)
                    e.then_inc(x1n_done, 1)

            def normalise_y(c, label, n):
                act.wait_ge(shift_done[3], c * 2 + (2 * label + n + 1))
                for i in range(2):
                    t = 2 * n + i
                    e = normalise(3, yo[:, t, :], yo[:, t, :], t)
                e.then_inc(y_norm, 1)

            def body_of(c, body):
                slots, _ = planned(body)
                for n in range(SLOTS):
                    if body != FIRST or n:
                        prob_high(c, n - 1)
                    exp(c, n)
                    if n:
                        for (label, (kind, k)), _, _ in slots[n - 1]:
                            if kind == "down" and k % 2:
                                normalise_y(c, label, k // 2)
                    for plan in sorted(slots[n], key=lambda plan: plan[0][1][0] == "wo"):
                        if plan[0][1][0] != "down":
                            item(c, plan)
                    if n == 6 and body != FIRST:
                        normalise_x1(c)

            act.wait_ge(ld_w["small"], 96)
            for name in WSEQ[:3]:
                split_weight(name)
            for i, plan in enumerate(prologue):
                if i == 5:
                    split_weight("wq1")
                item(-1, plan)
            for name in WSEQ[4:]:
                split_weight(name)
            over_chunks(act, body_of)
            prob_high(NC - 1, SLOTS - 1)
            for plan in epilogue:
                kind, n = plan[0][1]
                if kind != "down":
                    item(NC, plan)
                    if (kind, n) == ("wo", 1):
                        normalise_x1(NC)
                elif n % 2:
                    normalise_y(NC, LAST, n // 2)

        @block.vector
        def _(dve):
            V = nc.vector

            def maxima(c, n):
                dve.wait_ge(s_done, sets(c, n))
                V.tensor_reduce(nmax[:, n % 2, :].rearrange("p (b r) -> p b r", b=2),
                                ps_s[:, :, 0:2 * KEYS].rearrange("p b (r k) -> p b r k", r=2),
                                AX_X, ALU.max, negate=True).then_inc(max_done, 1)

            def prob_low(c, m):
                dve.wait_ge(ph_done, sets(c, m))
                V.scalar_tensor_tensor(p_hl[1][:, m % 2, :], ps_t[:, 0:5 * P], PSCALE, p_hl[0][:, m % 2, :],
                                       ALU.mult, ALU.subtract).then_inc(pl_done, 1)

            def sum_parts(c, m, body):
                m = m % SLOTS if m >= 0 else m
                g, s = divmod(m % SLOTS, NG)
                dve.wait_ge(pv_done, sets(c, m))
                if s == 0 and not (body == FIRST and m == 0):
                    dve.wait_ge(o_done, c * NG + (m // NG))
                V.tensor_reduce(osum[:, s, :, :], ps_v.rearrange("p (k a n) -> p k n a", k=4, a=3),
                                AX_X, ALU.add).then_inc(os_done, 1)

            def normalise_heads(c, m, body):
                m = m % SLOTS if m >= 0 else m
                g, s = divmod(m % SLOTS, NG)
                if s < NG - 1:
                    return
                dve.wait_ge(os_done, sets(c, m))
                all16 = osum[:, :, :, :].rearrange("p s k n -> p (s k) n")
                V.reciprocal(rsum[:, :].unsqueeze(2), all16[:, :, DV:DV + 1]).then_inc(r_done, 1)
                dve.wait_ge(r_done, c * NG + (m // NG + 1))
                if g == 0 and body != FIRST:
                    dve.wait_ge(done["ot"], count(c, LAST, "ot", 1))
                V.tensor_tensor(oall[:, :, g * 32:(g + 1) * 32].rearrange("p b (r d) -> p b r d", r=2),
                                all16[:, :, 0:DV].rearrange("p (b r) d -> p b r d", r=2),
                                rsum[:, :].rearrange("p (b r) -> p b r", r=2).unsqueeze(3).broadcast_to([P, BLK, 2, DV]),
                                ALU.mult).then_inc(o_done, 1)

            def ln_stats(i, srcs, t0, before):
                q, n = ln_step[i], len(srcs)
                for t, src in enumerate(srcs):
                    e = V.bn_stats(st[:, i, t0 + t, :], src)
                e.then_inc(q, 1)
                held(dve, q, before + 1)
                for t in range(n):
                    e = V.bn_aggr(mv[:, i, t0 + t, :], st[:, i, t0 + t, :])
                e.then_inc(q, 1)
                dve.wait_ge(q, before + 2)
                V.tensor_scalar(minus_mean[:, i, t0:t0 + n].unsqueeze(2), mv[:, i, t0:t0 + n, 0:1], -1.0, None,
                                ALU.mult)
                V.tensor_scalar(vareps[:, i, t0:t0 + n].unsqueeze(2), mv[:, i, t0:t0 + n, 1:2], EPS, None,
                                ALU.add).then_inc(q, 1)

            def stats_x(c, label):
                dve.wait_ge(ld_x, c * 16 + 16 * (label + 1))
                ln_stats(0, [xa[:, t, :] for t in range(4)], 0, c * LN + LN * label)

            def normalise_x(c, label):
                dve.wait_ge(rstd_done[0], c + (label + 1))
                for t in range(4):
                    e = V.tensor_scalar(xa[:, t, :], xa[:, t, :], mv[:, 0, t, 0:1], rstd[:, 0, t:t + 1],
                                        ALU.subtract, ALU.mult)
                e.then_inc(xn_done, 1)

            def stats_x1(c):
                for f in range(2):
                    dve.wait_ge(x1_done, c * 2 + (2 * LAST + f + 1))
                    ln_stats(2, [x1[:, 2 * f + i, :] for i in range(2)], 2 * f, c * (2 * LN) + (2 * LAST + f) * LN)

            def split_weight(name):
                i = WSEQ.index(name)
                dve.wait_ge(w_hi, i + 1)
                for src, parts in weight(name):
                    e = V.tensor_tensor(parts[1], src, parts[0], ALU.subtract)
                e.then_inc(w_lo, 1)

            def dequant(n):
                q, w = (up_q, down_q)[n], deq.bitcast(I32)
                dve.wait_ge(ld_w[("upq", "downq")[n]], 16)
                dve.wait_ge(ld_w["small"], 96)
                tiles, sc = ((HC, scu), (KC, scd))[n]
                wide = 2048 // tiles
                for k in range(tiles):
                    v = w[:, k * wide:(k + 1) * wide].rearrange("p (b n) -> p b n", n=QBLK)
                    o = deq[:, k * wide:(k + 1) * wide].rearrange("p (b n) -> p b n", n=QBLK)
                    e = V.scalar_tensor_tensor(o, v, -7.5, sc[:, k, :].unsqueeze(2).broadcast_to([P, wide // QBLK, QBLK]),
                                               ALU.add, ALU.mult)
                e.then_inc(deq_done, 1)

            def cosines(c, label, n, bank):
                dve.wait_ge(swapped, count(c, label, "rope", n))
                if n == 0:
                    dve.wait_ge(ld_cs, c * 16 + 16 * (label + 1))
                if not (isinstance(c, int) and c + label == 0 and n < 2):
                    dve.wait_ge(rot_done, count(c, label, "rope", n - 2))
                V.tensor_tensor(straight[:, n % 2, :], ring[bank][:, :], cs[:, 0, :], ALU.mult
                                ).then_inc(taken["rope"], 1)

            def rotate(c, label, n):
                tile = ROPE_ORDER[n]
                g = tile[1]
                dve.wait_ge(sin_done, count(c, label, "rope", n))
                dve.wait_ge(taken["rope"], count(c, label, "rope", n))
                if n - 1 in ON_POOL:
                    dve.wait_ge(rot_done, count(c, label, "rope", n - 1))
                first = isinstance(c, int) and c + label == 0
                if tile[0] == "q":
                    if not (first and g < 2):
                        dve.wait_ge(s_done, c * SLOTS + (label * SLOTS + NG * g - NG))
                    V.tensor_tensor(*rotated_queries(n), ALU.add).then_inc(rot_done, 1)
                    return
                k4 = c * (4 * NG) + (label * 4 * NG + 4 * g)
                own = kwin[:, g, :, WIN:2 * WIN]
                if not first:
                    dve.wait_ge(s_done, c * SLOTS + (label * SLOTS - SLOTS + NG * g + NG))
                    V.tensor_copy(kwin[:, g, 0, 0:WIN], own[:, BLK - 1, :]).then_inc(k_step, 1)
                else:
                    V.memset(kwin[:, g, 0, 0:WIN], 0.0).then_inc(k_step, 1)
                if not (first and g == 0):
                    dve.wait_ge(k_step, k4)
                V.tensor_tensor(kfront[:, :], straight[:, n % 2, 0:FRONT], turned[:, n % 2, 0:FRONT], ALU.add
                                ).then_inc(k_step, 1)
                dve.wait_ge(k_step, k4 + 2)
                half = half_of(c, label)
                if isinstance(c, int):
                    to = kwin[:, g, :, (2 - half) * WIN:(2 - half) * WIN + FRONT]
                else:
                    to = kwin[:, g, :, bass.ds(half * (-WIN) + 2 * WIN, FRONT)]
                V.tensor_scalar(to, kfront[:, :].unsqueeze(1).broadcast_to([P, BLK, FRONT]), 1.0, None, ALU.mult
                                ).then_inc(k_step, 1)
                dve.wait_ge(k_step, k4 + 3)
                V.tensor_tensor(own, straight[:, n % 2, :].rearrange("p (b n) -> p b n", n=WIN),
                                turned[:, n % 2, :].rearrange("p (b n) -> p b n", n=WIN), ALU.add
                                ).then_inc(rot_done, 1)
                dve.wait_ge(rot_done, count(c, label, "rope", n))
                V.tensor_copy(kwin[:, g, 1:BLK, 0:WIN], own[:, 0:BLK - 1, :]).then_inc(k_step, 1)

            def item(c, plan):
                (label, (kind, n)), bank, _ = plan
                ps = ring[bank]
                if kind == "rope":
                    cosines(c, label, n, bank)
                elif kind in ("xn", "ot", "xa", "wu", "wd"):
                    dve.wait_ge(high[kind], count(c, label, kind, n))
                    parts, src = hi_lo(kind, n, bank)
                    V.tensor_tensor(parts[1], src, parts[0], ALU.subtract).then_inc(taken[kind], 1)
                elif kind == "vw":
                    dve.wait_ge(high["vw"], count(c, label, kind, n))
                    if not (isinstance(c, int) and c == 0):
                        dve.wait_ge(v_wide, c * 2)
                    else:
                        dve.wait_ge(zeroed, 1)
                    rest, part = value_parts()
                    V.tensor_tensor(rest, ps[:, :].rearrange("p (w g d) -> p w g d", g=NG, d=DV), part[0],
                                    ALU.subtract).then_inc(taken["vw"], 1)
                elif kind == "vf":
                    dve.wait_ge(high["vf"], count(c, label, kind, n))
                    V.tensor_tensor(vfrest[:, :], ps[:, 0:64], vfp[:, 0, :], ALU.subtract).then_inc(taken["vf"], 1)
                elif kind == "wo":
                    dve.wait_ge(done["wo"], count(c, label, kind, n))
                    ln_stats(1, [ps[:, i * D:(i + 1) * D] for i in range(2)], 2 * n, count(c, label, kind, n - 1) * LN)
                elif kind == "up":
                    dve.wait_ge(taken["up"], count(c, label, kind, n))
                    V.tensor_copy(x2_hl[0][:, 2 * (n % 4):2 * (n % 4) + 2, :],
                                  x2f[:, n % 2, :].rearrange("p (k n) -> p k n", k=2)).then_inc(x2h_done, 1)
                elif kind == "down":
                    dve.wait_ge(done["down"], count(c, label, kind, n))
                    f, i = divmod(n, 2)
                    if i == 0:
                        dve.wait_ge(stored[f], c * 16 + (16 * label + 16))
                    V.tensor_tensor(yo[:, n, :], ps[:, 0:D], bdn[:, :], ALU.add).then_inc(taken["down"], 1)
                    if i == 1:
                        dve.wait_ge(taken["down"], count(c, label, kind, n))
                        ln_stats(3, [yo[:, 2 * f + i, :] for i in range(2)], 2 * f, c * (2 * LN) + (2 * label + f) * LN)

            def front_values(c):
                b = c * 5
                dve.wait_ge(taken["vf"], count(c, NOW, "vf", 0))
                V.tensor_copy(vfp[:, 1, :], vfrest[:, :]).then_inc(v_step, 1)
                dve.wait_ge(v_step, b + 1)
                V.tensor_tensor(vfp[:, 2, :], vfrest[:, :], vfp[:, 1, :], ALU.subtract).then_inc(v_step, 1)
                dve.wait_ge(v_step, b + 2)
                half = half_of(c, NOW)
                for t in range(4):
                    rows = slice(32 * t, 32 * t + 32)
                    if isinstance(c, int):
                        to = vdiag[rows, half, :, t * VP:(t + 1) * VP]
                    else:
                        to = vdiag[rows, bass.ds(half, 1), :, t * VP:(t + 1) * VP].rearrange("p a g n -> p (a g) n")
                    e = V.tensor_scalar(to.rearrange("p g (a n) -> p g a n", a=3)[:, :, :, 0:DV],
                                        vfp[rows, :, :].rearrange("p a (g d) -> p g a d", g=NG), 1.0, None, ALU.mult)
                e.then_inc(v_step, 3)

            waiting = []

            def flush(c, keep=0):
                while len(waiting) > keep:
                    label, n = waiting.pop(0)
                    if n not in ON_POOL:
                        rotate(c, label, n)

            def items(c, plans):
                for plan in plans:
                    label, (kind, n) = plan[0]
                    if kind == "rope":
                        flush(c, 1)
                        waiting.append((label, n))
                    item(c, plan)

            def body_of(c, body):
                waiting[:] = [(NOW, n) for _, (kind, n) in JOBS[SLOTS - 1] if kind == "rope"]
                slots, _ = planned(body)
                for n in range(SLOTS):
                    maxima(c, n)
                    if body != FIRST or n:
                        prob_low(c, n - 1)
                    if n == 2:
                        front_values(c)
                    flush(c)
                    if body != FIRST or n >= 3:
                        normalise_heads(c, n - 3, body)
                    if n == 8 and body != FINAL:
                        stats_x(c, NEXT)
                    if n == 9 and body != FINAL:
                        normalise_x(c, NEXT)
                    if body == FIRST and n == 4:
                        dequant(0)
                    if body == FIRST and n == 9:
                        dequant(1)
                    at = min(values_after(n, slots[n]), max(len(slots[n]) - 1, 0))
                    items(c, slots[n][:at])
                    if body != FIRST or n >= 2:
                        sum_parts(c, n - 2, body)
                    items(c, slots[n][at:])
                    if n == 5 and body != FIRST:
                        stats_x1(c)
                if body == FIRST:
                    dve.wait_ge(done["wd"], 4)
                    dve.sem_inc(x1_free, 1)

            V.memset(vwin[:, :, :, :], 0.0).then_inc(fill_step, 1)
            dve.wait_ge(fill_step, 1)
            V.memset(vwin[:, :, :, DV:DV + 1], 1.0)
            V.memset(minus_half[:, :], -0.5)
            V.memset(vdiag[:, :, :, :], 0.0)
            V.memset(vt[:, 0:WIN], 0.0).then_inc(fill_step, 1)
            dve.wait_ge(fill_step, 2)
            for t in range(4):
                e = V.memset(vdiag[32 * t:32 * t + 32, :, :, t * VP + DV:t * VP + DV + 1], 1.0)
            e.then_inc(zeroed, 1)
            stats_x(-1, NEXT)
            normalise_x(-1, NEXT)
            for name in WSEQ[:3]:
                split_weight(name)
            items(-1, prologue[:5])
            split_weight("wq1")
            items(-1, prologue[5:])
            flush(-1, sum(kind == "rope" for _, (kind, _) in JOBS[SLOTS - 1]))
            for name in WSEQ[4:]:
                split_weight(name)
            over_chunks(dve, body_of)
            prob_low(NC - 1, SLOTS - 1)
            sum_parts(NC - 1, SLOTS - 2, FINAL)
            sum_parts(NC - 1, SLOTS - 1, FINAL)
            normalise_heads(NC - 1, SLOTS - 1, FINAL)
            for plan in epilogue:
                item(NC, plan)
                if plan[0][1] == ("wo", 1):
                    stats_x1(NC)

        @block.gpsimd
        def _(pool):
            G = nc.gpsimd

            def item(c, plan):
                label, (kind, n) = plan[0]
                if kind == "rope":
                    pool.wait_ge(swapped, count(c, label, "rope", n))
                    if n == 0:
                        pool.wait_ge(ld_cs, c * 16 + 16 * (label + 1))
                    G.tensor_tensor(turned[:, n % 2, :], turned[:, n % 2, :], cs[:, 1, :], ALU.mult
                                    ).then_inc(sin_done, 1)
                elif kind == "up":
                    pool.wait_ge(x2h_done, count(c, label, kind, n))
                    k = 2 * (n % 4)
                    G.tensor_tensor(x2_hl[1][:, k:k + 2, :], x2f[:, n % 2, :].rearrange("p (k n) -> p k n", k=2),
                                    x2_hl[0][:, k:k + 2, :], ALU.subtract).then_inc(x2l_done, 1)
                elif kind == "down" and n % 2:
                    power(3, n - 1, 2, c * 2 + (2 * label + n // 2))
                elif kind == "wo":
                    power(1, 2 * n, 2, count(c, label, kind, n - 1))

            def residual(c, plan):
                label, (kind, n) = plan[0]
                if n == 0:
                    pool.wait_ge(ld_x1, c * 16 + 16 * (label + 1))
                pool.wait_ge(taken["wo"], count(c, label, kind, n))
                G.tensor_tensor(x1[:, 2 * n:2 * n + 2, :], x1[:, 2 * n:2 * n + 2, :], zn[:, 2 * n:2 * n + 2, :],
                                ALU.add).then_inc(x1_done, 1)

            def power(i, t0, n, before):
                pool.wait_ge(ln_step[i], before * LN + LN)
                G.tensor_tensor(rstd[:, i, t0:t0 + n], vareps[:, i, t0:t0 + n], minus_half[:, 0:n], ALU.pow
                                ).then_inc(rstd_done[i], 1)
                pool.wait_ge(rstd_done[i], before + 1)
                G.tensor_tensor(nmr[:, i, t0:t0 + n], minus_mean[:, i, t0:t0 + n], rstd[:, i, t0:t0 + n], ALU.mult
                                ).then_inc(shift_done[i], 1)

            def power_x(c, label):
                power(0, 0, 4, c + label)

            def power_x1(c):
                for f in range(2):
                    power(2, 2 * f, 2, c * 2 + (2 * LAST + f))

            def gather_front(c, n):
                pool.wait_ge(exp_done, sets(c, n))
                if not (isinstance(c, int) and c == 0 and n == 0):
                    pool.wait_ge(t_done, sets(c, n - 1))
                pool.sem_inc(gates[pool.engine], 1)
                G.tensor_copy(pfront[:, :].rearrange("p (k n) -> p k n", k=4), prob[:, :, P:KEYS]
                              ).then_inc(pf_done, 1)

            def rotate(c, label, n):
                g = ROPE_ORDER[n][1]
                pool.wait_ge(sin_done, count(c, label, "rope", n))
                pool.wait_ge(taken["rope"], count(c, label, "rope", n))
                pool.wait_ge(rot_done, count(c, label, "rope", n - 1))
                if g >= 2 or not (isinstance(c, int) and c + label == 0):
                    pool.wait_ge(s_done, c * SLOTS + (label * SLOTS + NG * g - NG))
                G.tensor_tensor(*rotated_queries(n), ALU.add).then_inc(rot_done, 1)

            def window_values(c):
                rest, part = value_parts()
                held(pool, taken["vw"], count(c, NOW, "vw", 0))
                G.tensor_copy(part[1], rest).then_inc(v_wide, 1)
                pool.wait_ge(v_wide, c * 2 + 1)
                G.tensor_tensor(part[2], rest, part[1], ALU.subtract).then_inc(v_wide, 1)

            def finish(c, label, n):
                pool.wait_ge(y_norm, c * 2 + (2 * label + n + 1))
                G.tensor_tensor(yo[:, 2 * n:2 * n + 2, :], yo[:, 2 * n:2 * n + 2, :], x1[:, 2 * n:2 * n + 2, :],
                                ALU.add).then_inc(x1_free, 1)

            def body_of(c, body):
                slots, _ = planned(body)
                for n in range(SLOTS):
                    if n:
                        for (label, (kind, k)), _, _ in slots[n - 1]:
                            if kind == "rope" and k in ON_POOL:
                                rotate(c, label, k)
                    if n == 2:
                        window_values(c)
                    gather_front(c, n)
                    if body == FIRST and n == 2:
                        pool.wait_ge(w_lo, len(WSEQ))
                        pool.wait_ge(v_wide, 2)
                        G.memset(scratch[:, 2048:4608], 0.0).then_inc(padded, 1)
                    if n:
                        for (label, (kind, k)), _, _ in slots[n - 1]:
                            if kind == "down" and k % 2:
                                finish(c, label, k // 2)
                    if n == 8 and body != FINAL:
                        power_x(c, NEXT)
                    for plan in slots[n]:
                        item(c, plan)
                    if n == 5 and body != FIRST:
                        power_x1(c)
                    for plan in slots[n]:
                        if plan[0][1][0] == "wo":
                            residual(c, plan)

            pool.wait_ge(zeroed, 1)
            power_x(-1, NEXT)
            for plan in prologue:
                item(-1, plan)
            over_chunks(pool, body_of)
            for plan in epilogue:
                item(NC, plan)
                kind, n = plan[0][1]
                if kind == "wo":
                    residual(NC, plan)
                    if n == 1:
                        power_x1(NC)
                if kind == "down" and n % 2:
                    finish(NC, LAST, n // 2)


def constants():
    freq = (1.0 / THETA ** (np.arange(0, DQK, 2)[:DQK // 2].astype(np.float32) / DQK)).astype(np.float32)
    ang = np.outer(np.arange(S, dtype=np.float32), freq).T
    scale = np.float32(float(DQK) ** -0.25)
    cos, sin = np.cos(ang) * scale, np.sin(ang) * scale
    tables = np.stack([np.concatenate([cos, cos]), np.concatenate([-sin, sin])], 1)
    tables = tables.reshape(P, 2, HALVES, CH).transpose(2, 0, 1, 3)
    q = np.arange(P) % WIN
    half_masks = []
    for blk in range(3):
        row = WIN * blk + q[:, None]
        band_keys = WIN * (blk - 1) + np.arange(2 * WIN)[None, :]
        band = (band_keys >= 0) & (band_keys <= row) & (band_keys > row - WIN)
        front_keys = np.arange(FRONT)[None, :]
        front = front_keys <= row - WIN
        ok = np.concatenate([band, front], 1)
        half_masks.append(np.tile(np.where(ok, 0.0, MASKED), (1, 2)))
    mask01 = np.stack([np.stack([half_masks[0], half_masks[1]], 1), np.stack([half_masks[2]] * 2, 1)])
    return (np.ascontiguousarray(tables, dtype=np.float32), mask01, half_masks[2], np.eye(P))


_INS = ["L0_attn_x", "L0_attn_wq", "L0_attn_wk", "L0_attn_wv", "L0_attn_wo", "L0_ffn_w_up_q",
        "L0_ffn_w_up_scale", "L0_ffn_b_up", "L0_ffn_w_up_lora_a", "L0_ffn_w_up_lora_b", "L0_ffn_w_down_q",
        "L0_ffn_w_down_scale", "L0_ffn_b_down", "L0_ffn_w_down_lora_a", "L0_ffn_w_down_lora_b"]


def kernel(**inputs):
    import concourse.bacc as bacc
    from concourse.bass_utils import run_bass_kernel_spmd

    tables, mask01, mask2, eye = constants()
    bf16 = np.dtype("bfloat16")
    arrays = {name: np.ascontiguousarray(inputs[name]) for name in _INS}
    arrays |= {"tables": tables, "mask01": mask01.astype(bf16), "mask2": mask2.astype(bf16),
               "ident32": eye.astype(np.float32), "ident16": eye.astype(bf16)}
    nc = bacc.Bacc("TRN2", target_bir_lowering=False, num_devices=1)
    args = [nc.dram_tensor(f"in_{k}", a.shape, mybir.dt.from_np(a.dtype), kind="ExternalInput").ap()
            for k, a in arrays.items()]
    out = nc.dram_tensor("out", (B, S, D), F32, kind="ExternalOutput").ap()
    build(nc, *args, out)
    r = run_bass_kernel_spmd(nc, [{f"in_{k}": a for k, a in arrays.items()}], core_ids=[0])
    return r.results[0]["out"]
```

```python
from contextlib import ExitStack

import numpy as np

import concourse.bass as bass
from concourse import mybir

F32 = mybir.dt.float32
F32R = mybir.dt.float32r
F16 = mybir.dt.float16
BF16 = mybir.dt.bfloat16
I32 = mybir.dt.int32
ALU = mybir.AluOpType
ACT = mybir.ActivationFunctionType
AX_X = mybir.AxisListType.X

P = 128
B, S, D = 4, 1024, 256
NH, NG, DQK, DV = 16, 4, 128, 16
REP = NH // NG
WIN, FRONT = 64, 32
HID, RANK = 1024, 16
QBLK = 64
THETA = 10000.0
EPS = 1e-5
CH = 512
NC = B * S // CH
HALVES = S // CH
KC = D // P
HC = HID // P
BLK = CH // WIN
KEYS = 2 * WIN + FRONT
SLOTS = NG * BLK // 2
VP = 3 * (DV + 1)
PSCALE = 2.0 ** 14
MASKED = -1e30
ROPES = NG * (REP + 1)

PER_CHUNK = {"rope": ROPES, "vt": 1, "vw": 1, "vf": 1, "ot": 2, "wo": 2, "xa": 2, "up": 8,
             "down": 4, "xn": 2, "wt": 3, "wu": 4, "wd": 4}


def rope(*tile):
    return ("rope", tile)


NOW, NEXT, LAST, SETUP = 0, 1, -1, "setup"
JOBS = {
    0: [(NOW, rope("q", 1, 1)), (NOW, rope("q", 1, 2))],
    1: [(NOW, rope("q", 1, 3)), (NOW, ("vw", 0)), (NOW, ("vf", 0))],
    2: [(NOW, rope("q", 2, 1)), (NOW, rope("q", 2, 0))],
    3: [(LAST, ("ot", 0)), (LAST, ("ot", 1)), (NOW, rope("q", 2, 2))],
    4: [(LAST, ("wo", 0)), (LAST, ("wo", 1)), (NOW, rope("k", 2))],
    5: [(NOW, rope("q", 2, 3))],
    6: [(NOW, rope("q", 3, 0)), (NOW, rope("q", 3, 1))],
    7: [(LAST, ("xa", 0)), (LAST, ("xa", 1)), (NOW, rope("k", 3))],
    8: [(LAST, ("up", 0)), (LAST, ("up", 1)), (NOW, rope("q", 3, 2))],
    9: [(LAST, ("up", 2)), (LAST, ("up", 3)), (NOW, rope("q", 3, 3)), (NEXT, ("xn", 0))],
    10: [(NEXT, ("xn", 1)), (LAST, ("down", 0))],
    11: [(LAST, ("down", 1)), (NEXT, rope("q", 0, 0))],
    12: [(LAST, ("up", 4)), (NEXT, rope("q", 0, 1)), (LAST, ("up", 5)), (NEXT, rope("k", 0))],
    13: [(LAST, ("up", 6)), (LAST, ("up", 7)), (NEXT, rope("q", 0, 2))],
    14: [(LAST, ("down", 2)), (LAST, ("down", 3)), (NEXT, rope("q", 0, 3)), (NEXT, rope("k", 1))],
    15: [(NEXT, ("vt", 0)), (NEXT, rope("q", 1, 0))],
}
ROPE_ORDER = [job[1] for wanted in (NEXT, NOW) for n in range(SLOTS) for label, job in JOBS[n]
              if label == wanted and job[0] == "rope"]
ROPE_AT = {tile: n for n, tile in enumerate(ROPE_ORDER)}
JOBS = {n: [(label, (kind, ROPE_AT[k] if kind == "rope" else k)) for label, (kind, k) in jobs]
        for n, jobs in JOBS.items()}
VALUES_AFTER = {0: 3, 5: 1, 11: 2}
READ_OUT_AFTER = {7: 0, 8: 0}
ON_POOL = [ROPE_AT[tile] for tile in [
    ("q", 2, 0), ("q", 2, 2), ("q", 2, 3), ("q", 3, 0), ("q", 3, 1), ("q", 3, 2),
    ("q", 3, 3)]]
SETUP_JOBS = {4: [("wt", 0), ("wt", 1), ("wt", 2)], 6: [("wu", 0)], 7: [("wu", 1)], 8: [("wu", 2)],
              9: [("wu", 3)], 11: [("wd", 0)], 12: [("wd", 1)], 13: [("wd", 2)], 14: [("wd", 3)]}
PROLOGUE = [job for n in range(SLOTS) for job in JOBS[n] if job[0] == NEXT]
EPILOGUE = [(LAST, (kind, n)) for kind, n in [("ot", 0), ("wo", 0), ("ot", 1), ("wo", 1), ("xa", 0)]
            + [("up", n) for n in range(4)] + [("xa", 1), ("down", 0), ("down", 1)]
            + [("up", n) for n in range(4, 8)] + [("down", 2), ("down", 3)]]
BANKS = 4
LN = 3
FIRST, MIDDLE, FINAL = "first", "middle", "final"


def jobs_of(body, slot):
    found = [j for j in JOBS[slot] if not (body == FIRST and j[0] == LAST)
             and not (body == FINAL and j[0] == NEXT)]
    if body == FIRST:
        found = [(SETUP, j) for j in SETUP_JOBS.get(slot, [])] + found
    return found


def plan_banks(jobs, before):
    n, plan = len(jobs), []
    held = dict(enumerate(before))
    for i, job in enumerate(jobs):
        bank = (i - n) % BANKS
        plan.append((job, bank, held.get(bank)))
        held[bank] = job
    return plan, [held[b] for b in range(BANKS)]


def older(jobs):
    return [(label if label == SETUP else label - 1, job) for label, job in jobs]


def build(nc, x, wq, wk, wv, wo, up_q, up_scale, b_up, up_a, up_b, down_q, down_scale, b_down,
          down_a, down_b, tables, mask01, mask2, ident32, ident16, out):
    ctx = ExitStack()
    with ctx:
        def sb(name, shape, dt=F32):
            return ctx.enter_context(nc.sbuf_tensor(name, shape, dt))

        def sem(name):
            return ctx.enter_context(nc.semaphore(name))

        wq_hl = [sb(f"wq_{p}", [P, KC, NH * DQK], F32R) for p in "hl"]
        wk_hl = [sb(f"wk_{p}", [P, KC, NG * DQK], F32R) for p in "hl"]
        wv_hl = [sb(f"wv_{p}", [P, KC, NG * DV], F32R) for p in "hl"]
        wo_hl = [sb(f"wo_{p}", [P, 2, D], F32R) for p in "hl"]
        wup_hl = [sb(f"wup_{p}", [P, KC, HID], F32R) for p in "hl"]
        wdn_hl = [sb(f"wdn_{p}", [P, HC, D], F32R) for p in "hl"]
        id32 = sb("id32", [P, P])
        id16 = sb("id16", [P, P], BF16)
        bup = sb("bup", [P, HC])
        bdn = sb("bdn", [P, D])
        scu = sb("scu", [P, HC, D // QBLK])
        scd = sb("scd", [P, KC, HID // QBLK])
        cs = sb("cs", [P, 2, CH])
        m01 = sb("m01", [P, 2, 2 * KEYS], BF16)
        m2 = sb("m2", [P, 2 * KEYS], BF16)
        xa = sb("xa", [P, 4, D])
        xt_hl = [sb(f"xt_{p}", [P, KC, CH], F32R) for p in "hl"]
        turned = sb("turned", [P, 2, CH])
        straight = sb("straight", [P, 2, CH])
        qrot = sb("qrot", [P, 2, BLK, REP, WIN])
        kwin = sb("kwin", [P, NG, BLK, KEYS])
        kfront = sb("kfront", [P, FRONT])
        vt = sb("vt", [4 * DV, WIN + CH])
        vtf = sb("vtf", [4 * DV, 4 * FRONT])
        vwin = sb("vwin", [P, BLK, NG, VP], BF16)
        vfrest = sb("vfrest", [P, 4 * DV])
        vfp = sb("vfp", [P, 3, 4 * DV], BF16)
        vdiag = sb("vdiag", [P, 2, NG, 4 * VP], BF16)
        nmax = sb("nmax", [P, 2, 4])
        prob = sb("prob", [P, 4, KEYS])
        pfront = sb("pfront", [P, 4 * FRONT])
        p_hl = [sb(f"p_{p}", [P, 2, 5 * P], F16) for p in "hl"]
        osum = sb("osum", [P, 4, 4, DV + 1])
        rsum = sb("rsum", [P, 16])
        oall = sb("oall", [P, BLK, P])
        ot_hl = [sb(f"ot_{p}", [P, 2, CH], F32R) for p in "hl"]
        x2_hl = [sb(f"x2_{p}", [P, HC, CH // 2], F32R) for p in "hl"]
        scratch = sb("scratch", [P, 4608])
        zn = scratch[:, 0:1024].rearrange("p (t d) -> p t d", t=4)
        x1 = scratch[:, 1024:2048].rearrange("p (t d) -> p t d", t=4)
        yo = scratch[:, 2048:3072].rearrange("p (t d) -> p t d", t=4)
        x2f = scratch[:, 3072:4096].rearrange("p (b n) -> p b n", b=2)
        vrest = scratch[:, 4096:4608]
        wq_st = scratch[:, 0:2048].rearrange("p (b k n) -> p b k n", b=2, k=KC)
        wk_st = scratch[:, 2048:3072].rearrange("p (k n) -> p k n", k=KC)
        wv_st = scratch[:, 3072:3200].rearrange("p (k n) -> p k n", k=KC)
        wo_st = scratch[:, 3200:3712].rearrange("p (k n) -> p k n", k=2)
        deq = scratch[:, 0:2048]
        upb_st = scratch[:, 2048:3072]
        dnb_st = scratch[:, 3072:3328]
        upa_t = scratch[:, 3328:3584]
        dna_t = scratch[:, 3584:4608]
        upa_st = sb("upa_st", [P, KC, RANK])
        dna_st = sb("dna_st", [P, HC, RANK])
        st = sb("st", [P, 4, 4, 6])
        mv = sb("mv", [P, 4, 4, 2])
        vareps = sb("vareps", [P, 4, 4])
        rstd = sb("rstd", [P, 4, 4])
        minus_half = sb("minus_half", [P, 4])
        minus_mean = sb("minus_mean", [P, 4, 4])
        nmr = sb("nmr", [P, 4, 4])

        ring = [ctx.enter_context(nc.psum_tensor(f"ring{b}", [P, CH], F32)) for b in range(BANKS)]
        ps_s = ctx.enter_context(nc.psum_tensor("ps_s", [P, 2, 512], F32))
        ps_t = ctx.enter_context(nc.psum_tensor("ps_t", [P, 1024], F32))
        ps_v = ps_t[:, 5 * P:5 * P + 4 * VP]

        done = {k: sem(f"{k}_done") for k in PER_CHUNK}
        high = {k: sem(f"{k}_high") for k in ("xn", "ot", "xa", "wu", "wd", "vw", "vf")}
        taken = {k: sem(f"{k}_taken") for k in PER_CHUNK}
        swapped = sem("halves_swapped")
        sin_done = sem("sines_applied")
        rot_done = sem("tiles_rotated")
        k_step = sem("key_steps")
        s_done = sem("scores_done")
        max_done = sem("maxima_done")
        exp_done = sem("exp_done")
        pf_done = sem("front_probs_gathered")
        t_done = sem("prob_transposed")
        ph_done = sem("prob_high_done")
        pl_done = sem("prob_low_done")
        pv_done = sem("pv_done")
        os_done = sem("pv_summed")
        r_done = sem("sums_inverted")
        o_done = sem("heads_normalised")
        v_carry = sem("value_carried")
        v_wide = sem("value_window_parts")
        v_step = sem("front_value_parts")
        ln_step = [sem(f"ln{i}_steps") for i in range(4)]
        rstd_done = [sem(f"ln{i}_rstd") for i in range(4)]
        shift_done = {i: sem(f"ln{i}_shift") for i in (1, 2, 3)}
        xn_done = sem("x_normalised")
        z_done = sem("attention_normalised")
        x1_done = sem("x1_done")
        x1n_done = sem("x1_normalised")
        x2h_done = sem("hidden_high_done")
        x2l_done = sem("hidden_low_done")
        y_norm = sem("network_normalised")
        x1_free = sem("x1_free")
        stored = [sem(f"stored{i}") for i in range(2)]
        ld_x = sem("x_loaded")
        ld_x1 = sem("x_reloaded")
        ld_cs = sem("tables_loaded")
        ld_m = sem("masks_loaded")
        ld_w = {k: sem(f"{k}_loaded") for k in ("wk", "wq0", "wq1", "wq2", "wq3", "wv", "wo", "ident", "mask",
                                                 "small", "upq", "downq", "rank")}
        w_hi = sem("weights_high")
        w_lo = sem("weights_low")
        fill_step = sem("fill_steps")
        gates = {e.engine: sem(f"gate{i}") for i, e in enumerate((nc.tensor, nc.vector, nc.gpsimd))}
        zeroed = sem("zeroed")
        padded = sem("factors_zeroed")
        deq_done = sem("dequantised")
        WSEQ = ["wk", "wq0", "wv", "wq1", "wq2", "wq3", "wo"]

        x_v = x.rearrange("b (c t p) d -> (b c) p t d", p=P, t=4)
        out_v = out.rearrange("b (c f t p) d -> (b c) f p t d", p=P, f=2, t=2)

        before_job = [{0: "wk", 2: "wq0", 6: "wv", 7: "wq1"}.get(i) for i in range(len(PROLOGUE))]
        after_slot = {0: "wq2", 1: "wq3", 2: "wo"}

        def count(c, label, kind, n):
            if label == SETUP:
                return n + 1
            per = PER_CHUNK[kind]
            return c * per + (label * per + n + 1)

        def half_of(c, label):
            return (c + label) % HALVES

        def sets(c, n):
            return c * SLOTS + (n + 1)

        def over_chunks(e, body_of):
            body_of(0, FIRST)
            with e.Fori(1, NC - 1) as c:
                body_of(c, MIDDLE)
            body_of(NC - 1, FINAL)

        def planned(body):
            jobs = [j for n in range(SLOTS) for j in jobs_of(body, n)]
            plan, tail = plan_banks(jobs, older(PROLOGUE[-BANKS:]))
            by_slot, at = [], 0
            for n in range(SLOTS):
                k = len(jobs_of(body, n))
                by_slot.append(plan[at:at + k])
                at += k
            return by_slot, tail

        prologue = plan_banks(PROLOGUE, [None] * BANKS)[0]
        tail = planned(FINAL)[1]
        epilogue = plan_banks(EPILOGUE, older(tail))[0]

        def values_after(n, jobs):
            if n == 1:
                return 1
            if n in VALUES_AFTER and len(jobs) >= VALUES_AFTER[n]:
                return VALUES_AFTER[n]
            work = sum({"ot": 1, "xa": 1, "xn": 1, "down": 6}.get(plan[0][1][0], 3) for plan in jobs[:-1])
            return len(jobs) - 1 if work >= 6 else len(jobs)

        def held(e, q, value):
            e.wait_ge(q, value)
            e.sem_inc(gates[e.engine], 1)

        block = ctx.enter_context(nc.Block())

        @block.sync
        def _(sp):
            def load_x(c, waited):
                if waited:
                    sp.wait_ge(done["xn"], count(c, NOW, "xn", 1))
                    sp.dma_start(xa[:, :, :], x_v[bass.ds(c + 1, 1)].rearrange("a p t d -> p (a t) d")).then_inc(ld_x, 16)
                else:
                    sp.dma_start(xa[:, :, :], x_v[0]).then_inc(ld_x, 16)

            def load_tables(c, label):
                src = tables[bass.ds(half_of(c, label), 1)] if not isinstance(c, int) else \
                    tables[half_of(c, label):half_of(c, label) + 1]
                sp.dma_start(cs[:, :, :], src.rearrange("a p t n -> p (a t) n")).then_inc(ld_cs, 16)

            def load_masks(c, label):
                src = mask01[bass.ds(half_of(c, label), 1)] if not isinstance(c, int) else \
                    mask01[half_of(c, label):half_of(c, label) + 1]
                sp.dma_start(m01[:, :, :], src.rearrange("a p t n -> p (a t) n")).then_inc(ld_m, 16)

            def load_wq(g):
                if g >= 2:
                    sp.wait_ge(w_lo, WSEQ.index(f"wq{g - 2}") + 1)
                sp.dma_start(wq_st[:, g % 2, :, :],
                             wq.rearrange("(k p) n -> p k n", p=P)[:, :, g * 512:(g + 1) * 512]
                             ).then_inc(ld_w[f"wq{g}"], 16)

            def store(c, f):
                sp.wait_ge(x1_free, c * 2 + (f - 2 + 2))
                at = out_v[bass.ds(c - 1, 1), f].rearrange("a p t d -> p (a t) d")
                sp.dma_start(at, yo[:, 2 * f:2 * f + 2, :]).then_inc(stored[f], 16)

            def setup_loads():
                for q in stored:
                    sp.sem_inc(q, 16)
                load_x(0, False)
                sp.dma_start(id32[:, :], ident32).then_inc(ld_w["ident"], 16)
                sp.dma_start(wk_st, wk.rearrange("(k p) n -> p k n", p=P)).then_inc(ld_w["wk"], 16)
                load_wq(0)
                load_tables(0, NOW)
                sp.dma_start(wv_st, wv.rearrange("(k p) n -> p k n", p=P)).then_inc(ld_w["wv"], 16)
                load_masks(0, NOW)
                sp.dma_start(id16[:, :], ident16).then_inc(ld_w["mask"], 16)
                sp.dma_start(m2[:, :], mask2).then_inc(ld_w["mask"], 16)
                load_wq(1)
                for hh in range(2):
                    sp.dma_start(wo_st[:, hh, :], wo.rearrange("(a hh d) n -> hh a d n", hh=2, d=DV)[hh]
                                 ).then_inc(ld_w["wo"], 16)
                sp.dma_start(bup[:, :], b_up.rearrange("(k p) -> p k", p=P), allow_slow_non_contiguous=True
                             ).then_inc(ld_w["small"], 16)
                sp.dma_start(bdn[:, :], b_down.rearrange("(a n) -> a n", a=1).broadcast_to([P, D])).then_inc(ld_w["small"], 16)
                sp.dma_start(scu[:, :, :], up_scale.rearrange("(k p) n -> p k n", p=P)).then_inc(ld_w["small"], 16)
                sp.dma_start(scd[:, :, :], down_scale.rearrange("(k p) n -> p k n", p=P)).then_inc(ld_w["small"], 16)
                sp.dma_start(upa_st[:, :, :], up_a.rearrange("(k p) n -> p k n", p=P)).then_inc(ld_w["small"], 16)
                sp.dma_start(dna_st[:, :, :], down_a.rearrange("(k p) n -> p k n", p=P)).then_inc(ld_w["small"], 16)
                load_wq(2)
                load_wq(3)

            def setup_loads_late():
                sp.wait_ge(w_lo, len(WSEQ))
                sp.dma_start(deq.bitcast(I32).rearrange("p (k n) -> p k n", k=HC),
                             up_q.rearrange("(k p) n -> p k n", p=P)).then_inc(ld_w["upq"], 16)
                sp.wait_ge(padded, 1)
                sp.dma_start(upb_st[0:RANK, :], up_b).then_inc(ld_w["rank"], 16)
                sp.dma_start(dnb_st[0:RANK, :], down_b).then_inc(ld_w["rank"], 16)

            def setup_loads_last():
                sp.wait_ge(done["wu"], 4)
                sp.dma_start(deq.bitcast(I32).rearrange("p (k n) -> p k n", k=KC),
                             down_q.rearrange("(k p) n -> p k n", p=P)).then_inc(ld_w["downq"], 16)

            def body_of(c, body):
                if body != FINAL:
                    load_x(c, True)
                if body == FIRST:
                    setup_loads_late()
                    setup_loads_last()
                else:
                    sp.wait_ge(x1_free, c * 2 - 1)
                    sp.dma_start(x1, x_v[bass.ds(c - 1, 1)].rearrange("a p t d -> p (a t) d")
                                 ).then_inc(ld_x1, 16)
                if body != FINAL:
                    sp.wait_ge(taken["rope"], count(c, NOW, "rope", ROPES - 1))
                    sp.wait_ge(sin_done, count(c, NOW, "rope", ROPES - 1))
                    load_tables(c, NEXT)
                if body != FIRST:
                    store(c, 0)
                if body != FINAL:
                    sp.wait_ge(s_done, sets(c, SLOTS - 4))
                    load_masks(c, NEXT)
                if body != FIRST:
                    store(c, 1)

            setup_loads()
            over_chunks(sp, body_of)
            sp.wait_ge(x1_free, NC * 2 - 1)
            sp.dma_start(x1, x_v[NC - 1]).then_inc(ld_x1, 16)
            store(NC, 0)
            store(NC, 1)
            for q in stored:
                sp.wait_ge(q, 16 * (NC + 1))

        @block.tensor
        def _(pe):
            PASSES = ((0, 0), (0, 1), (1, 0))

            def claim(c, before):
                if before is not None:
                    label, (kind, n) = before
                    held(pe, taken[kind], count(c, label, kind, n))

            def scores(c, n, body):
                g, s = divmod(n, NG)
                if s == 0:
                    pe.wait_ge(k_step, c * (4 * NG) + 4 * g + 4)
                    pe.wait_ge(rot_done, count(c, NOW, "rope", ROPE_AT[("q", g, REP - 1)]))
                if n == 0:
                    pe.wait_ge(ld_m, c * 16 + 16)
                if body != FIRST or n:
                    pe.wait_ge(exp_done, sets(c, n - 1))
                else:
                    pe.wait_ge(ld_w["mask"], 32)
                for bb in range(2):
                    blk = 2 * s + bb
                    mask = m01[:, bb, :] if s == 0 else m2[:, :]
                    pe.matmul(ps_s[:, bb, 0:2 * KEYS], id16[:, :], mask, start=True, stop=False,
                              skip_group_check=True)
                    for pr in range(2):
                        mm = pe.matmul(ps_s[:, bb, pr * KEYS:(pr + 1) * KEYS],
                                       qrot[:, g % 2, blk, 2 * pr:2 * pr + 2, :].rearrange("p r q -> p (r q)"),
                                       kwin[:, g, blk, :],
                                       start=False, stop=True, skip_group_check=True)
                mm.then_inc(s_done, 1)

            def transposes(c, m, body):
                pe.wait_ge(exp_done, sets(c, m))
                if body != FIRST or m:
                    pe.wait_ge(pl_done, sets(c, m - 1))
                for k in range(4):
                    pe.transpose(ps_t[:, k * P:(k + 1) * P], prob[:, k, 0:P], id32[:, :])
                pe.wait_ge(pf_done, sets(c, m))
                if body != FIRST or m >= 2:
                    pe.wait_ge(os_done, sets(c, m - 2))
                pe.transpose(ps_t[:, 4 * P:5 * P], pfront[:, :], id32[:, :]).then_inc(t_done, 1)

            def values(c, m, body):
                g, s = divmod(m % SLOTS, NG)
                last = body == FINAL and m == SLOTS - 1
                pe.wait_ge(pl_done, sets(c, m if last else m + 1))
                if last:
                    pe.wait_ge(os_done, sets(c, m - 1))
                if m == 0:
                    pe.wait_ge(v_wide, c * 2 + 2)
                    pe.wait_ge(v_step, c * 5 + 5)
                lo = 2 * (DV + 1)
                ph, pl = (t[:, m % 2, :] for t in p_hl)
                diag = vdiag[:, 0, g, :]
                pe.matmul(ps_v, ph[:, 4 * P:5 * P], diag, start=True, stop=False,
                          skip_group_check=True)
                pe.matmul(ps_v.rearrange("p (k n) -> p k n", n=VP)[:, :, 0:lo], pl[:, 4 * P:5 * P],
                          diag.rearrange("p (k n) -> p k n", n=VP)[:, :, 0:lo], start=False, stop=False,
                          skip_group_check=True)
                for k in range(4):
                    w = vwin[:, 2 * s + k // 2, g, :]
                    pe.matmul(ps_v[:, k * VP:(k + 1) * VP], ph[:, k * P:(k + 1) * P], w,
                              start=False, stop=False, skip_group_check=True)
                    mm = pe.matmul(ps_v[:, k * VP:k * VP + lo], pl[:, k * P:(k + 1) * P], w[:, 0:lo],
                                   start=False, stop=True, skip_group_check=True)
                mm.then_inc(pv_done, 1)

            def three_passes(to, terms, first=True, last=True):
                for i, (a, b) in enumerate(terms):
                    for j, (pa, pb) in enumerate(PASSES):
                        mm = pe.matmul(to, a[pa], b[pb], start=first and i == 0 and j == 0,
                                       stop=last and i == len(terms) - 1 and j == len(PASSES) - 1)
                return mm

            def job(c, plan):
                (label, (kind, n)), bank, before = plan
                claim(c, before)
                to = ring[bank]
                if kind == "rope":
                    tile = ROPE_ORDER[n]
                    if n == 0:
                        pe.wait_ge(taken["xn"], count(c, label, "xn", KC - 1))
                    if isinstance(c, int) and c + label == 0:
                        name = "wk" if tile[0] == "k" else f"wq{tile[1]}"
                        pe.wait_ge(w_lo, WSEQ.index(name) + 1)
                    if tile[0] == "k":
                        w, at = wk_hl, tile[1] * DQK
                    else:
                        w, at = wq_hl, (tile[1] * REP + tile[2]) * DQK
                    mm = three_passes(to[:, :], [([t[:, k, at:at + DQK] for t in w], [t[:, k, :] for t in xt_hl])
                                                 for k in range(KC)])
                elif kind == "xn":
                    pe.wait_ge(xn_done, c * 1 + (label + 1))
                    if isinstance(c, int) and c < 0:
                        pe.wait_ge(ld_w["ident"], 16)
                    for t in range(4):
                        mm = pe.transpose(to[:, t * P:(t + 1) * P], xa[:, t, n * P:(n + 1) * P], id32[:, :])
                elif kind == "vt":
                    if isinstance(c, int) and c < 0:
                        pe.wait_ge(w_lo, WSEQ.index("wv") + 1)
                    mm = three_passes(to[0:NG * DV, :], [([t[:, k, :] for t in wv_hl], [t[:, k, :] for t in xt_hl])
                                                         for k in range(KC)])
                elif kind == "vw":
                    held(pe, taken["vt"], count(c, label, "vt", 0))
                    for w in range(BLK):
                        mm = pe.transpose(to[:, w * 64:(w + 1) * 64], vt[:, w * WIN:(w + 2) * WIN],
                                          id32[0:64, 0:64])
                elif kind == "vf":
                    mm = pe.transpose(to[:, 0:64], vtf[:, :], id32[0:64, 0:64])
                elif kind == "ot":
                    pe.wait_ge(o_done, c * NG + (label + 1) * NG + (n if isinstance(c, int) and c == NC else 0))
                    for b in range(4):
                        mm = pe.transpose(to[:, b * P:(b + 1) * P], oall[:, 4 * n + b, :], id32[:, :])
                elif kind == "wo":
                    pe.wait_ge(taken["ot"], count(c, label, "ot", n))
                    for i in range(2):
                        t = 2 * n + i
                        mm = three_passes(to[:, i * D:(i + 1) * D],
                                          [([o[:, hh, t * P:(t + 1) * P] for o in ot_hl], [w[:, hh, :] for w in wo_hl])
                                           for hh in range(2)])
                elif kind == "xa":
                    pe.wait_ge(x1n_done, c * 2 + (2 * label + n + 1))
                    for k in range(KC):
                        for i in range(2):
                            mm = pe.transpose(to[:, (2 * k + i) * P:(2 * k + i + 1) * P],
                                              zn[:, 2 * n + i, k * P:(k + 1) * P], id32[:, :])
                elif kind == "up":
                    f, h0 = n // 4, 2 * (n % 4)
                    if n % 4 == 0:
                        pe.wait_ge(taken["xa"], count(c, label, "xa", f))
                    for i in range(2):
                        at = (h0 + i) * P
                        mm = three_passes(to[:, i * 256:(i + 1) * 256],
                                          [([w[:, k, at:at + P] for w in wup_hl],
                                            [o[:, k, f * 256:(f + 1) * 256] for o in ot_hl]) for k in range(KC)])
                elif kind == "down":
                    f, i = divmod(n, 2)
                    for k in range(0, HC, 2):
                        if i == 0:
                            pe.wait_ge(x2l_done, count(c, label, "up", 4 * f + k // 2))
                        mm = three_passes(to[:, 0:D], [([o[:, j, i * P:(i + 1) * P] for o in x2_hl],
                                                        [w[:, j, :] for w in wdn_hl]) for j in (k, k + 1)],
                                          first=k == 0, last=k == HC - 2)
                elif kind == "wt":
                    pe.wait_ge(ld_w["small"], 96)
                    blocks = [upa_st[:, k, :] for k in range(KC)] if n == 0 else \
                        [dna_st[:, 4 * (n - 1) + k, :] for k in range(4)]
                    for i, a in enumerate(blocks):
                        mm = pe.transpose(to[0:RANK, i * P:(i + 1) * P], a, id32[:, :])
                elif kind == "wu":
                    if n == 0:
                        pe.wait_ge(taken["wt"], 3)
                        pe.wait_ge(ld_w["rank"], 32)
                        pe.wait_ge(deq_done, 1)
                    k, hh = n // 2, n % 2
                    pe.matmul(to[:, :], upa_t[:, k * P:(k + 1) * P], upb_st[:, hh * 512:(hh + 1) * 512],
                              start=True, stop=False, skip_group_check=True)
                    for i in range(4):
                        t = deq.rearrange("p (k n) -> p k n", k=HC)[:, 4 * hh + i, k * P:(k + 1) * P]
                        mm = pe.matmul(to[:, i * P:(i + 1) * P], t, id32[:, :], start=False, stop=True,
                                       skip_group_check=True)
                elif kind == "wd":
                    if n == 0:
                        pe.wait_ge(deq_done, 2)
                    for i in range(2):
                        h = 2 * n + i
                        pe.matmul(to[:, i * D:(i + 1) * D], dna_t[:, h * P:(h + 1) * P], dnb_st[:, :],
                                  start=i == 0, stop=False, skip_group_check=True)
                        for o in range(KC):
                            t = deq.rearrange("p (k n) -> p k n", k=KC)[:, o, h * P:(h + 1) * P]
                            mm = pe.matmul(to[:, i * D + o * P:i * D + (o + 1) * P], t, id32[:, :],
                                           start=False, stop=True, skip_group_check=True)
                mm.then_inc(done[kind], 1)

            def body_of(c, body):
                slots, _ = planned(body)
                for n in range(SLOTS):
                    scores(c, n, body)
                    if body != FIRST or n >= 1:
                        transposes(c, n - 1, body)
                    jobs = slots[n]
                    at = values_after(n, jobs)
                    for plan in jobs[:at]:
                        job(c, plan)
                    if body != FIRST or n >= 2:
                        values(c, n - 2, body)
                    for plan in jobs[at:]:
                        job(c, plan)

            for plan in prologue:
                job(-1, plan)
            over_chunks(pe, body_of)
            transposes(NC - 1, SLOTS - 1, FINAL)
            for i, plan in enumerate(epilogue):
                if 1 <= i < 3:
                    values(NC - 1, SLOTS - 3 + i, FINAL)
                job(NC, plan)

        def hi_lo(kind, n, bank):
            to = ring[bank][:, :]
            if kind == "xn":
                return [t[:, n, :] for t in xt_hl], to
            if kind == "xa":
                return [t[:, :, n * 256:(n + 1) * 256] for t in ot_hl], to.rearrange("p (k n) -> p k n", k=KC)
            if kind == "ot":
                return [t[:, :, n * 256:(n + 1) * 256].rearrange("p h (b q) -> p b h q", q=WIN) for t in ot_hl], \
                    to.rearrange("p (b h q) -> p b h q", b=4, h=2)
            if kind == "wu":
                return [t[:, n // 2, (n % 2) * 512:(n % 2 + 1) * 512] for t in wup_hl], to
            return [t[:, 2 * n:2 * n + 2, :] for t in wdn_hl], to.rearrange("p (k n) -> p k n", k=2)

        def value_parts():
            return vrest.rearrange("p (w g d) -> p w g d", g=NG, d=DV), \
                [vwin[:, :, :, i * (DV + 1):i * (DV + 1) + DV] for i in range(3)]

        def hidden_parts(n):
            k = 2 * (n % 4)
            return [t[:, k:k + 2, :] for t in x2_hl], x2f[:, n % 2, :].rearrange("p (k n) -> p k n", k=2)

        def rotated_queries(n):
            _, g, h = ROPE_ORDER[n]
            return [qrot[:, g % 2, :, h, :]] + [t[:, n % 2, :].rearrange("p (b n) -> p b n", n=WIN)
                                                for t in (straight, turned)]

        def weight(name):
            if name[:2] == "wv":
                return [(wv_st[:, k, :], [t[:, k, :] for t in wv_hl]) for k in range(KC)]
            if name[:2] == "wo":
                return [(wo_st[:, k, :], [t[:, k, :] for t in wo_hl]) for k in range(2)]
            if name[:2] == "wk":
                src, parts, at = wk_st, wk_hl, 0
            else:
                g = int(name[2])
                src, parts, at = wq_st[:, g % 2, :, :], wq_hl, g * 512
            return [(src[:, k, :].rearrange("p (h f t) -> p h t f", h=4, t=2),
                     [t[:, k, at:at + 512].rearrange("p (h t f) -> p h t f", h=4, t=2) for t in parts])
                    for k in range(KC)]

        @block.scalar
        def _(act):
            def exp(c, n):
                act.wait_ge(max_done, sets(c, n))
                if not (isinstance(c, int) and c == 0 and n == 0):
                    act.wait_ge(t_done, sets(c, n - 1))
                for k in range(4):
                    e = nc.scalar.activation(prob[:, k, :],
                                             ps_s[:, k // 2, (k % 2) * KEYS:(k % 2 + 1) * KEYS],
                                             ACT.Exp, bias=nmax[:, n % 2, k:k + 1])
                e.then_inc(exp_done, 1)

            def prob_high(c, m):
                act.wait_ge(t_done, sets(c, m))
                nc.scalar.activation(p_hl[0][:, m % 2, :], ps_t[:, 0:5 * P], ACT.Copy, scale=PSCALE
                                     ).then_inc(ph_done, 1)

            def split_weight(name):
                i = WSEQ.index(name)
                act.wait_ge(ld_w[name], 32 if name == "wo" else 16)
                for src, parts in weight(name):
                    e = nc.scalar.activation(parts[0], src, ACT.Copy)
                e.then_inc(w_hi, 1)

            def item(c, plan):
                (label, (kind, n)), bank, _ = plan
                ps = ring[bank]
                act.wait_ge(done[kind], count(c, label, kind, n))
                if kind == "rope":
                    if not (isinstance(c, int) and c + label == 0 and n < 2):
                        act.wait_ge(rot_done, count(c, label, kind, n - 2))
                    nc.scalar.activation(turned[0:64, n % 2, :], ps[64:128, :], ACT.Copy)
                    nc.scalar.activation(turned[64:128, n % 2, :], ps[0:64, :], ACT.Copy).then_inc(swapped, 1)
                elif kind == "vt":
                    if isinstance(c, int) and c < 0:
                        act.wait_ge(zeroed, 1)
                    else:
                        nc.scalar.activation(vt[:, 0:WIN], vt[:, CH:CH + WIN], ACT.Copy).then_inc(v_carry, 1)
                        act.wait_ge(v_carry, c + (label + 0))
                    nc.scalar.activation(vtf[:, :].rearrange("p (k n) -> p k n", k=4),
                                         ps[0:64, 0:FRONT].unsqueeze(1).broadcast_to([64, 4, FRONT]), ACT.Copy)
                    nc.scalar.activation(vt[:, WIN:], ps[0:64, :], ACT.Copy).then_inc(taken["vt"], 1)
                elif kind == "vw":
                    nc.scalar.activation(vwin[:, :, :, 0:DV], ps[:, :].rearrange("p (w g d) -> p w g d", g=NG, d=DV),
                                         ACT.Copy).then_inc(high["vw"], 1)
                elif kind == "vf":
                    nc.scalar.activation(vfp[:, 0, :], ps[:, 0:64], ACT.Copy).then_inc(high["vf"], 1)
                elif kind == "wo":
                    act.wait_ge(shift_done[1], count(c, label, "wo", n))
                    for i in range(2):
                        e = normalise(1, zn[:, 2 * n + i, :], ps[:, i * D:(i + 1) * D], 2 * n + i)
                    e.then_inc(taken["wo"], 1)
                elif kind == "up":
                    if n >= 2:
                        act.wait_ge(x2l_done, count(c, label, kind, n - 2))
                    for i in range(2):
                        h = 2 * (n % 4) + i
                        e = nc.scalar.activation(x2f[:, n % 2, i * 256:(i + 1) * 256], ps[:, i * 256:(i + 1) * 256],
                                                 ACT.Relu, bias=bup[:, h:h + 1])
                    e.then_inc(taken["up"], 1)
                elif kind == "wt":
                    act.wait_ge(padded, 1)
                    if n == 0:
                        nc.scalar.activation(upa_t[0:RANK, :], ps[0:RANK, 0:256], ACT.Copy).then_inc(taken["wt"], 1)
                    else:
                        nc.scalar.activation(dna_t[0:RANK, (n - 1) * 512:n * 512], ps[0:RANK, :], ACT.Copy
                                             ).then_inc(taken["wt"], 1)
                else:
                    parts, src = hi_lo(kind, n, bank)
                    nc.scalar.activation(parts[0], src, ACT.Copy).then_inc(high[kind], 1)

            def normalise(i, to, src, t):
                return nc.scalar.activation(to, src, ACT.Identity, bias=nmr[:, i, t:t + 1], scale=rstd[:, i, t:t + 1])

            def normalise_x1(c, f):
                act.wait_ge(shift_done[2], c * 2 + (2 * LAST + f + 1))
                for t in (2 * f, 2 * f + 1):
                    e = normalise(2, zn[:, t, :], x1[:, t, :], t)
                e.then_inc(x1n_done, 1)

            def normalise_y(c, label, n):
                act.wait_ge(shift_done[3], c * 2 + (2 * label + n + 1))
                for i in range(2):
                    t = 2 * n + i
                    e = normalise(3, yo[:, t, :], yo[:, t, :], t)
                e.then_inc(y_norm, 1)

            def body_of(c, body):
                slots, _ = planned(body)
                for n in range(SLOTS):
                    if body != FIRST or n:
                        prob_high(c, n - 1)
                    exp(c, n)
                    if n:
                        for (label, (kind, k)), _, _ in slots[n - 1]:
                            if kind == "down" and k % 2:
                                normalise_y(c, label, k // 2)
                    for plan in sorted(slots[n], key=lambda plan: plan[0][1] == ("wo", 1)):
                        if plan[0][1][0] != "down":
                            item(c, plan)
                    if body == FIRST and n in after_slot:
                        split_weight(after_slot[n])
                    if n == 6 and body != FIRST:
                        normalise_x1(c, 0)
                        normalise_x1(c, 1)

            for plan, name in zip(prologue, before_job):
                if name:
                    split_weight(name)
                item(-1, plan)
            act.wait_ge(ld_w["small"], 96)
            over_chunks(act, body_of)
            prob_high(NC - 1, SLOTS - 1)
            for plan in epilogue:
                kind, n = plan[0][1]
                if (kind, n) == ("wo", 1):
                    normalise_x1(NC, 0)
                if kind != "down":
                    item(NC, plan)
                if (kind, n) == ("xa", 0):
                    normalise_x1(NC, 1)
                if (kind, n) in (("up", 7), ("down", 3)):
                    normalise_y(NC, LAST, int(kind == "down"))

        @block.vector
        def _(dve):
            V = nc.vector

            def maxima(c, n):
                dve.wait_ge(s_done, sets(c, n))
                V.tensor_reduce(nmax[:, n % 2, :].rearrange("p (b r) -> p b r", b=2),
                                ps_s[:, :, 0:2 * KEYS].rearrange("p b (r k) -> p b r k", r=2),
                                AX_X, ALU.max, negate=True).then_inc(max_done, 1)

            def prob_low(c, m):
                dve.wait_ge(ph_done, sets(c, m))
                V.scalar_tensor_tensor(p_hl[1][:, m % 2, :], ps_t[:, 0:5 * P], PSCALE, p_hl[0][:, m % 2, :],
                                       ALU.mult, ALU.subtract).then_inc(pl_done, 1)

            def sum_parts(c, m, body):
                m = m % SLOTS if m >= 0 else m
                g, s = divmod(m % SLOTS, NG)
                dve.wait_ge(pv_done, sets(c, m))
                if s == 0 and not (body == FIRST and m == 0):
                    dve.wait_ge(o_done, c * NG + (m // NG))
                V.tensor_reduce(osum[:, s, :, :], ps_v.rearrange("p (k a n) -> p k n a", k=4, a=3),
                                AX_X, ALU.add).then_inc(os_done, 1)

            def normalise_heads(c, m, body):
                m = m % SLOTS if m >= 0 else m
                g, s = divmod(m % SLOTS, NG)
                by_halves = body == FINAL and m // NG == NG - 1
                if s < NG - 1 and not (by_halves and s == 1):
                    return
                dve.wait_ge(os_done, sets(c, m))
                s0 = NG // 2 if by_halves and s == NG - 1 else 0
                outs, blocks = slice(4 * s0, 4 * s + 4), slice(2 * s0, 2 * s + 2)
                some = osum[:, :, :, :].rearrange("p s k n -> p (s k) n")[:, outs, :]
                V.reciprocal(rsum[:, outs].unsqueeze(2), some[:, :, DV:DV + 1]).then_inc(r_done, 1)
                dve.wait_ge(r_done, c * NG + (m // NG + 1 + (s0 > 0)))
                if g == 0 and body != FIRST:
                    dve.wait_ge(done["ot"], count(c, LAST, "ot", 1))
                V.tensor_tensor(oall[:, blocks, g * 32:(g + 1) * 32].rearrange("p b (r d) -> p b r d", r=2),
                                some[:, :, 0:DV].rearrange("p (b r) d -> p b r d", r=2),
                                rsum[:, outs].rearrange("p (b r) -> p b r", r=2).unsqueeze(3).broadcast_to(
                                    [P, 2 * (s - s0 + 1), 2, DV]),
                                ALU.mult).then_inc(o_done, 1)

            def ln_stats(i, srcs, t0, before):
                q, n = ln_step[i], len(srcs)
                for t, src in enumerate(srcs):
                    e = V.bn_stats(st[:, i, t0 + t, :], src)
                e.then_inc(q, 1)
                held(dve, q, before + 1)
                for t in range(n):
                    e = V.bn_aggr(mv[:, i, t0 + t, :], st[:, i, t0 + t, :])
                e.then_inc(q, 1)
                dve.wait_ge(q, before + 2)
                if i in shift_done:
                    V.tensor_scalar(minus_mean[:, i, t0:t0 + n].unsqueeze(2), mv[:, i, t0:t0 + n, 0:1], -1.0, None,
                                    ALU.mult)
                V.tensor_scalar(vareps[:, i, t0:t0 + n].unsqueeze(2), mv[:, i, t0:t0 + n, 1:2], EPS, None,
                                ALU.add).then_inc(q, 1)

            def stats_x(c, label):
                dve.wait_ge(ld_x, c * 16 + 16 * (label + 1))
                ln_stats(0, [xa[:, t, :] for t in range(4)], 0, c * LN + LN * label)

            def normalise_x(c, label):
                dve.wait_ge(rstd_done[0], c + (label + 1))
                for t in range(4):
                    e = V.tensor_scalar(xa[:, t, :], xa[:, t, :], mv[:, 0, t, 0:1], rstd[:, 0, t:t + 1],
                                        ALU.subtract, ALU.mult)
                e.then_inc(xn_done, 1)

            def hidden_low(c, label, job):
                n = job[1]
                dve.wait_ge(x2h_done, count(c, label, "up", n))
                parts, src = hidden_parts(n)
                V.tensor_tensor(parts[1], src, parts[0], ALU.subtract).then_inc(x2l_done, 1)

            def stats_x1(c, f):
                dve.wait_ge(x1_done, c * 2 + (2 * LAST + f + 1))
                ln_stats(2, [x1[:, 2 * f + i, :] for i in range(2)], 2 * f, c * (2 * LN) + (2 * LAST + f) * LN)

            def split_weight(name):
                i = WSEQ.index(name)
                dve.wait_ge(w_hi, i + 1)
                for src, parts in weight(name):
                    e = V.tensor_tensor(parts[1], src, parts[0], ALU.subtract)
                e.then_inc(w_lo, 1)

            def dequant(n):
                q, w = (up_q, down_q)[n], deq.bitcast(I32)
                dve.wait_ge(ld_w[("upq", "downq")[n]], 16)
                dve.wait_ge(ld_w["small"], 96)
                tiles, sc = ((HC, scu), (KC, scd))[n]
                wide = 2048 // tiles
                for k in range(tiles):
                    v = w[:, k * wide:(k + 1) * wide].rearrange("p (b n) -> p b n", n=QBLK)
                    o = deq[:, k * wide:(k + 1) * wide].rearrange("p (b n) -> p b n", n=QBLK)
                    e = V.scalar_tensor_tensor(o, v, -7.5, sc[:, k, :].unsqueeze(2).broadcast_to([P, wide // QBLK, QBLK]),
                                               ALU.add, ALU.mult)
                e.then_inc(deq_done, 1)

            def cosines(c, label, n, bank):
                dve.wait_ge(swapped, count(c, label, "rope", n))
                if n == 0:
                    dve.wait_ge(ld_cs, c * 16 + 16 * (label + 1))
                if not (isinstance(c, int) and c + label == 0 and n < 2):
                    dve.wait_ge(rot_done, count(c, label, "rope", n - 2))
                V.tensor_tensor(straight[:, n % 2, :], ring[bank][:, :], cs[:, 0, :], ALU.mult
                                ).then_inc(taken["rope"], 1)

            def rotate(c, label, n):
                tile = ROPE_ORDER[n]
                g = tile[1]
                dve.wait_ge(sin_done, count(c, label, "rope", n))
                dve.wait_ge(taken["rope"], count(c, label, "rope", n))
                if n - 1 in ON_POOL:
                    dve.wait_ge(rot_done, count(c, label, "rope", n - 1))
                first = isinstance(c, int) and c + label == 0
                if tile[0] == "q":
                    if not (first and g < 2):
                        dve.wait_ge(s_done, c * SLOTS + (label * SLOTS + NG * g - NG))
                    V.tensor_tensor(*rotated_queries(n), ALU.add).then_inc(rot_done, 1)
                    return
                k4 = c * (4 * NG) + (label * 4 * NG + 4 * g)
                own = kwin[:, g, :, WIN:2 * WIN]
                if not first:
                    dve.wait_ge(s_done, c * SLOTS + (label * SLOTS - SLOTS + NG * g + NG))
                    V.tensor_copy(kwin[:, g, 0, 0:WIN], own[:, BLK - 1, :]).then_inc(k_step, 1)
                else:
                    V.memset(kwin[:, g, 0, 0:WIN], 0.0).then_inc(k_step, 1)
                if not (first and g == 0):
                    dve.wait_ge(k_step, k4)
                V.tensor_tensor(kfront[:, :], straight[:, n % 2, 0:FRONT], turned[:, n % 2, 0:FRONT], ALU.add
                                ).then_inc(k_step, 1)
                dve.wait_ge(k_step, k4 + 2)
                half = half_of(c, label)
                if isinstance(c, int):
                    to = kwin[:, g, :, (2 - half) * WIN:(2 - half) * WIN + FRONT]
                else:
                    to = kwin[:, g, :, bass.ds(half * (-WIN) + 2 * WIN, FRONT)]
                V.tensor_scalar(to, kfront[:, :].unsqueeze(1).broadcast_to([P, BLK, FRONT]), 1.0, None, ALU.mult
                                ).then_inc(k_step, 1)
                dve.wait_ge(k_step, k4 + 3)
                V.tensor_tensor(own, straight[:, n % 2, :].rearrange("p (b n) -> p b n", n=WIN),
                                turned[:, n % 2, :].rearrange("p (b n) -> p b n", n=WIN), ALU.add
                                ).then_inc(rot_done, 1)
                dve.wait_ge(rot_done, count(c, label, "rope", n))
                V.tensor_copy(kwin[:, g, 1:BLK, 0:WIN], own[:, 0:BLK - 1, :]).then_inc(k_step, 1)

            def item(c, plan):
                (label, (kind, n)), bank, _ = plan
                ps = ring[bank]
                if kind == "rope":
                    cosines(c, label, n, bank)
                elif kind in ("xn", "ot", "xa", "wu", "wd"):
                    dve.wait_ge(high[kind], count(c, label, kind, n))
                    parts, src = hi_lo(kind, n, bank)
                    V.tensor_tensor(parts[1], src, parts[0], ALU.subtract).then_inc(taken[kind], 1)
                elif kind == "vw":
                    dve.wait_ge(high["vw"], count(c, label, kind, n))
                    if not (isinstance(c, int) and c == 0):
                        dve.wait_ge(v_wide, c * 2)
                    else:
                        dve.wait_ge(zeroed, 1)
                    rest, part = value_parts()
                    V.tensor_tensor(rest, ps[:, :].rearrange("p (w g d) -> p w g d", g=NG, d=DV), part[0],
                                    ALU.subtract).then_inc(taken["vw"], 1)
                elif kind == "vf":
                    dve.wait_ge(high["vf"], count(c, label, kind, n))
                    V.tensor_tensor(vfrest[:, :], ps[:, 0:64], vfp[:, 0, :], ALU.subtract).then_inc(taken["vf"], 1)
                elif kind == "wo":
                    dve.wait_ge(done["wo"], count(c, label, kind, n))
                    ln_stats(1, [ps[:, i * D:(i + 1) * D] for i in range(2)], 2 * n, count(c, label, kind, n - 1) * LN)
                elif kind == "up":
                    dve.wait_ge(taken["up"], count(c, label, kind, n))
                    parts, src = hidden_parts(n)
                    V.tensor_copy(parts[0], src).then_inc(x2h_done, 1)
                elif kind == "down":
                    dve.wait_ge(done["down"], count(c, label, kind, n))
                    f, i = divmod(n, 2)
                    if i == 0:
                        dve.wait_ge(stored[f], c * 16 + (16 * label + 16))
                    V.tensor_tensor(yo[:, n, :], ps[:, 0:D], bdn[:, :], ALU.add).then_inc(taken["down"], 1)
                    if i == 1:
                        dve.wait_ge(taken["down"], count(c, label, kind, n))
                        ln_stats(3, [yo[:, 2 * f + i, :] for i in range(2)], 2 * f, c * (2 * LN) + (2 * label + f) * LN)

            def front_values(c):
                b = c * 5
                dve.wait_ge(taken["vf"], count(c, NOW, "vf", 0))
                V.tensor_copy(vfp[:, 1, :], vfrest[:, :]).then_inc(v_step, 1)
                dve.wait_ge(v_step, b + 1)
                V.tensor_tensor(vfp[:, 2, :], vfrest[:, :], vfp[:, 1, :], ALU.subtract).then_inc(v_step, 1)
                dve.wait_ge(v_step, b + 2)
                half = half_of(c, NOW)
                for t in range(4):
                    rows = slice(32 * t, 32 * t + 32)
                    if isinstance(c, int):
                        to = vdiag[rows, half, :, t * VP:(t + 1) * VP]
                    else:
                        to = vdiag[rows, bass.ds(half, 1), :, t * VP:(t + 1) * VP].rearrange("p a g n -> p (a g) n")
                    e = V.tensor_scalar(to.rearrange("p g (a n) -> p g a n", a=3)[:, :, :, 0:DV],
                                        vfp[rows, :, :].rearrange("p a (g d) -> p g a d", g=NG), 1.0, None, ALU.mult)
                e.then_inc(v_step, 3)

            waiting = []

            def flush(c, keep=0):
                while len(waiting) > keep:
                    label, n = waiting.pop(0)
                    if n not in ON_POOL:
                        rotate(c, label, n)

            def items(c, plans, keep=1):
                for plan in plans:
                    label, (kind, n) = plan[0]
                    if kind == "rope":
                        flush(c, keep)
                        waiting.append((label, n))
                    item(c, plan)

            def body_of(c, body):
                if body == FIRST:
                    waiting[:] = [(NOW, n) for _, n in waiting]
                else:
                    waiting[:] = [(NOW, n) for _, (kind, n) in JOBS[SLOTS - 1] if kind == "rope"]
                slots, _ = planned(body)
                for n in range(SLOTS):
                    maxima(c, n)
                    if body != FIRST or n:
                        prob_low(c, n - 1)
                    if n == 2:
                        front_values(c)
                    flush(c)
                    if body != FIRST or n >= 3:
                        normalise_heads(c, n - 3, body)
                    if n == 6 and body != FIRST:
                        stats_x1(c, 1)
                    if n == 7 and body != FINAL:
                        stats_x(c, NEXT)
                    if n == 9 and body != FINAL:
                        normalise_x(c, NEXT)
                    if body == FIRST and n == 5:
                        dequant(0)
                    if body == FIRST and n == 10:
                        dequant(1)
                    at = READ_OUT_AFTER.get(n, min(values_after(n, slots[n]), max(len(slots[n]) - 1, 0)))
                    items(c, slots[n][:at])
                    if body != FIRST or n >= 2:
                        sum_parts(c, n - 2, body)
                    items(c, slots[n][at:])
                    if body == FIRST and n in after_slot:
                        split_weight(after_slot[n])
                    if n == 5 and body != FIRST:
                        stats_x1(c, 0)
                if body == FIRST:
                    dve.wait_ge(done["wd"], 4)
                    dve.sem_inc(x1_free, 1)

            V.memset(vwin[:, :, :, :], 0.0).then_inc(fill_step, 1)
            dve.wait_ge(fill_step, 1)
            V.memset(vwin[:, :, :, DV:DV + 1], 1.0)
            V.memset(minus_half[:, :], -0.5)
            V.memset(vdiag[:, :, :, :], 0.0)
            V.memset(vt[:, 0:WIN], 0.0).then_inc(fill_step, 1)
            dve.wait_ge(fill_step, 2)
            for t in range(4):
                e = V.memset(vdiag[32 * t:32 * t + 32, :, :, t * VP + DV:t * VP + DV + 1], 1.0)
            e.then_inc(zeroed, 1)
            stats_x(-1, NEXT)
            normalise_x(-1, NEXT)
            for plan, name in zip(prologue, before_job):
                if name:
                    split_weight(name)
                items(-1, [plan], keep=0)
            over_chunks(dve, body_of)
            normalise_heads(NC - 1, SLOTS - 3, FINAL)
            prob_low(NC - 1, SLOTS - 1)
            for i, plan in enumerate(epilogue):
                if plan[0][1] == ("wo", 1):
                    stats_x1(NC, 0)
                item(NC, plan)
                if plan[0][1][0] == "up":
                    hidden_low(NC, *plan[0])
                if plan[0][1] == ("xa", 0):
                    stats_x1(NC, 1)
                if plan[0][1] in (("down", 2), ("down", 3)):
                    n = plan[0][1][1] - 2
                    dve.wait_ge(y_norm, NC * 2 + (2 * LAST + n + 1))
                    V.tensor_tensor(yo[:, 2 * n:2 * n + 2, :], yo[:, 2 * n:2 * n + 2, :], x1[:, 2 * n:2 * n + 2, :],
                                    ALU.add).then_inc(x1_free, 1)
                if i < 2:
                    sum_parts(NC - 1, SLOTS - 2 + i, FINAL)
                if i == 1:
                    normalise_heads(NC - 1, SLOTS - 1, FINAL)

        @block.gpsimd
        def _(pool):
            G = nc.gpsimd

            def item(c, plan):
                label, (kind, n) = plan[0]
                if kind == "rope":
                    pool.wait_ge(swapped, count(c, label, "rope", n))
                    if n == 0:
                        pool.wait_ge(ld_cs, c * 16 + 16 * (label + 1))
                    G.tensor_tensor(turned[:, n % 2, :], turned[:, n % 2, :], cs[:, 1, :], ALU.mult
                                    ).then_inc(sin_done, 1)
                elif kind == "up":
                    pool.wait_ge(x2h_done, count(c, label, kind, n))
                    parts, src = hidden_parts(n)
                    G.tensor_tensor(parts[1], src, parts[0], ALU.subtract).then_inc(x2l_done, 1)
                elif kind == "down" and n % 2:
                    power(3, n - 1, 2, c * 2 + (2 * label + n // 2))
                elif kind == "wo":
                    power(1, 2 * n, 2, count(c, label, kind, n - 1))

            def residual(c, plan):
                label, (kind, n) = plan[0]
                if n == 0:
                    pool.wait_ge(ld_x1, c * 16 + 16 * (label + 1))
                pool.wait_ge(taken["wo"], count(c, label, kind, n))
                G.tensor_tensor(x1[:, 2 * n:2 * n + 2, :], x1[:, 2 * n:2 * n + 2, :], zn[:, 2 * n:2 * n + 2, :],
                                ALU.add).then_inc(x1_done, 1)

            def power(i, t0, n, before):
                pool.wait_ge(ln_step[i], before * LN + LN)
                G.tensor_tensor(rstd[:, i, t0:t0 + n], vareps[:, i, t0:t0 + n], minus_half[:, 0:n], ALU.pow
                                ).then_inc(rstd_done[i], 1)
                if i in shift_done:
                    pool.wait_ge(rstd_done[i], before + 1)
                    G.tensor_tensor(nmr[:, i, t0:t0 + n], minus_mean[:, i, t0:t0 + n], rstd[:, i, t0:t0 + n], ALU.mult
                                    ).then_inc(shift_done[i], 1)

            def power_x(c, label):
                power(0, 0, 4, c + label)

            def power_x1(c, f):
                power(2, 2 * f, 2, c * 2 + (2 * LAST + f))

            def gather_front(c, n):
                pool.wait_ge(exp_done, sets(c, n))
                if not (isinstance(c, int) and c == 0 and n == 0):
                    pool.wait_ge(t_done, sets(c, n - 1))
                pool.sem_inc(gates[pool.engine], 1)
                G.tensor_copy(pfront[:, :].rearrange("p (k n) -> p k n", k=4), prob[:, :, P:KEYS]
                              ).then_inc(pf_done, 1)

            def rotate(c, label, n):
                g = ROPE_ORDER[n][1]
                pool.wait_ge(sin_done, count(c, label, "rope", n))
                pool.wait_ge(taken["rope"], count(c, label, "rope", n))
                pool.wait_ge(rot_done, count(c, label, "rope", n - 1))
                if g >= 2 or not (isinstance(c, int) and c + label == 0):
                    pool.wait_ge(s_done, c * SLOTS + (label * SLOTS + NG * g - NG))
                G.tensor_tensor(*rotated_queries(n), ALU.add).then_inc(rot_done, 1)

            def window_values(c):
                rest, part = value_parts()
                held(pool, taken["vw"], count(c, NOW, "vw", 0))
                G.tensor_copy(part[1], rest).then_inc(v_wide, 1)
                pool.wait_ge(v_wide, c * 2 + 1)
                G.tensor_tensor(part[2], rest, part[1], ALU.subtract).then_inc(v_wide, 1)

            def finish(c, label, n):
                pool.wait_ge(y_norm, c * 2 + (2 * label + n + 1))
                G.tensor_tensor(yo[:, 2 * n:2 * n + 2, :], yo[:, 2 * n:2 * n + 2, :], x1[:, 2 * n:2 * n + 2, :],
                                ALU.add).then_inc(x1_free, 1)

            def body_of(c, body):
                slots, _ = planned(body)
                for n in range(SLOTS):
                    if n:
                        for (label, (kind, k)), _, _ in slots[n - 1]:
                            if kind == "rope" and k in ON_POOL:
                                rotate(c, label, k)
                    if n == 2:
                        window_values(c)
                    gather_front(c, n)
                    if body == FIRST and n == 3:
                        pool.wait_ge(w_lo, len(WSEQ))
                        pool.wait_ge(v_wide, 2)
                        G.memset(scratch[:, 2048:4608], 0.0).then_inc(padded, 1)
                    if n:
                        for (label, (kind, k)), _, _ in slots[n - 1]:
                            if kind == "down" and k % 2:
                                finish(c, label, k // 2)
                    if n == 7 and body != FINAL:
                        power_x(c, NEXT)
                    if n == 6 and body != FIRST:
                        power_x1(c, 1)
                    for plan in slots[n]:
                        item(c, plan)
                    if n == 5 and body != FIRST:
                        power_x1(c, 0)
                    for plan in slots[n]:
                        if plan[0][1][0] == "wo":
                            residual(c, plan)

            pool.wait_ge(zeroed, 1)
            power_x(-1, NEXT)
            for plan in prologue:
                item(-1, plan)
            over_chunks(pool, body_of)
            for plan in epilogue:
                kind, n = plan[0][1]
                if kind != "up":
                    item(NC, plan)
                if kind == "wo":
                    residual(NC, plan)
                    power_x1(NC, n)


def constants():
    freq = (1.0 / THETA ** (np.arange(0, DQK, 2)[:DQK // 2].astype(np.float32) / DQK)).astype(np.float32)
    ang = np.outer(np.arange(S, dtype=np.float32), freq).T
    scale = np.float32(float(DQK) ** -0.25)
    cos, sin = np.cos(ang) * scale, np.sin(ang) * scale
    tables = np.stack([np.concatenate([cos, cos]), np.concatenate([-sin, sin])], 1)
    tables = tables.reshape(P, 2, HALVES, CH).transpose(2, 0, 1, 3)
    q = np.arange(P) % WIN
    half_masks = []
    for blk in range(3):
        row = WIN * blk + q[:, None]
        band_keys = WIN * (blk - 1) + np.arange(2 * WIN)[None, :]
        band = (band_keys >= 0) & (band_keys <= row) & (band_keys > row - WIN)
        front_keys = np.arange(FRONT)[None, :]
        front = front_keys <= row - WIN
        ok = np.concatenate([band, front], 1)
        half_masks.append(np.tile(np.where(ok, 0.0, MASKED), (1, 2)))
    mask01 = np.stack([np.stack([half_masks[0], half_masks[1]], 1), np.stack([half_masks[2]] * 2, 1)])
    return (np.ascontiguousarray(tables, dtype=np.float32), mask01, half_masks[2], np.eye(P))


_INS = ["L0_attn_x", "L0_attn_wq", "L0_attn_wk", "L0_attn_wv", "L0_attn_wo", "L0_ffn_w_up_q",
        "L0_ffn_w_up_scale", "L0_ffn_b_up", "L0_ffn_w_up_lora_a", "L0_ffn_w_up_lora_b", "L0_ffn_w_down_q",
        "L0_ffn_w_down_scale", "L0_ffn_b_down", "L0_ffn_w_down_lora_a", "L0_ffn_w_down_lora_b"]


def kernel(**inputs):
    import concourse.bacc as bacc
    from concourse.bass_utils import run_bass_kernel_spmd

    tables, mask01, mask2, eye = constants()
    bf16 = np.dtype("bfloat16")
    arrays = {name: np.ascontiguousarray(inputs[name]) for name in _INS}
    arrays |= {"tables": tables, "mask01": mask01.astype(bf16), "mask2": mask2.astype(bf16),
               "ident32": eye.astype(np.float32), "ident16": eye.astype(bf16)}
    nc = bacc.Bacc("TRN2", target_bir_lowering=False, num_devices=1)
    args = [nc.dram_tensor(f"in_{k}", a.shape, mybir.dt.from_np(a.dtype), kind="ExternalInput").ap()
            for k, a in arrays.items()]
    out = nc.dram_tensor("out", (B, S, D), F32, kind="ExternalOutput").ap()
    build(nc, *args, out)
    r = run_bass_kernel_spmd(nc, [{f"in_{k}": a for k, a in arrays.items()}], core_ids=[0])
    return r.results[0]["out"]
```
